# Optimizing a Trainium2 kernel written in Bass

```python
import numpy as np
import jax
import jax.numpy as jnp

def _softmax(x, axis=-1):
    return jax.nn.softmax(x, axis=axis)

def _gelu(x):
    return jax.nn.gelu(x, approximate=True)

def _silu(x):
    return jax.nn.silu(x)

def _sigmoid(x):
    return jax.nn.sigmoid(x)

def _layernorm(x, axis=-1, eps=1e-05):
    m = jnp.mean(x, axis=axis, keepdims=True)
    v = jnp.var(x, axis=axis, keepdims=True)
    return (x - m) / jnp.sqrt(v + eps)

def _scatter_add(tgt, idx, src, axis=0):
    return tgt.at[idx].add(src)

def _segment_sum(src, seg, n):
    return jax.ops.segment_sum(src, seg, n)
kernel_name = 'mk_gnn_ffn_d1_gnn_r16_91088a'

def setup_inputs(seed: int=0):
    np.random.seed(seed)
    _w = jnp.asarray

    def _rec_inputs():
        import jax
        import jax.numpy as jnp
        _gk = jax.random.key(seed)
        x = -0.0002117 + 1 * jax.random.normal(jax.random.fold_in(_gk, 1), (6250, 256), jnp.float32)
        src = jax.random.randint(jax.random.fold_in(_gk, 2), (100000,), 0, 6250, jnp.int32)
        dst = jnp.minimum((6250 * jax.random.uniform(jax.random.fold_in(_gk, 3), (100000,)) ** 2.0).astype(jnp.int32), 99999)
        _o = jnp.argsort(dst, stable=True)
        src = src[_o]
        dst = dst[_o]
        return (x, src, dst)
    x, src, dst = _rec_inputs()

    def _L0_gnn_setup():
        import jax, jax.numpy as jnp
        import numpy as np
        N = 6250
        E = 100000
        H, F_IN, F_OUT = (8, 256, 32)
        key = jax.random.key(seed)
        k1, k2, k3, k4, k5 = jax.random.split(key, 5)
        x = jax.random.normal(k1, (N, F_IN), dtype=jnp.float32)
        edge_index = jax.random.randint(k2, (2, E), 0, N, dtype=jnp.int64)
        W = jax.random.normal(k3, (H, F_IN, F_OUT), dtype=jnp.float32) * (1.0 / np.sqrt(F_IN))
        a_src = jax.random.normal(k4, (H, F_OUT, 1), dtype=jnp.float32) * 0.1
        a_dst = jax.random.normal(k5, (H, F_OUT, 1), dtype=jnp.float32) * 0.1
        return {'x': x, 'edge_index': edge_index, 'W': W, 'a_src': a_src, 'a_dst': a_dst}
    _L0_gnn_all = _L0_gnn_setup()
    _L0_gnn_in = {k: v for k, v in _L0_gnn_all.items() if k in ('W', 'a_src', 'a_dst')}
    del _L0_gnn_all

    def _L0_ffn_setup():
        import jax, jax.numpy as jnp
        import numpy as np
        B, S, H, F, E, K = (8, 256, 256, 512, 16, 2)
        EPS = 1e-05
        key = jax.random.key(seed)
        ks = jax.random.split(key, 9)
        sc = 0.02
        return {'x': jax.random.normal(ks[0], (B, S, H), dtype=jnp.float32), 'gate_w': jax.random.normal(ks[1], (H, E), dtype=jnp.float32) * sc, 'gate_b': jnp.zeros((E,), dtype=jnp.float32), 'w1': jax.random.normal(ks[2], (E, H, F), dtype=jnp.float32) * sc, 'b1': jnp.zeros((E, F), dtype=jnp.float32), 'w2': jax.random.normal(ks[3], (E, F, H), dtype=jnp.float32) * sc, 'b2': jnp.zeros((E, H), dtype=jnp.float32), 'gamma': jnp.ones((H,), dtype=jnp.float32), 'beta': jnp.zeros((H,), dtype=jnp.float32)}
    _L0_ffn_all = _L0_ffn_setup()
    _L0_ffn_in = {k: v for k, v in _L0_ffn_all.items() if k in ('gate_w', 'gate_b', 'w1', 'b1', 'w2', 'b2', 'gamma', 'beta')}
    del _L0_ffn_all
    return {'x': x, 'src': src, 'dst': dst, 'L0_gnn_W': _L0_gnn_in['W'], 'L0_gnn_a_src': _L0_gnn_in['a_src'], 'L0_gnn_a_dst': _L0_gnn_in['a_dst'], 'L0_ffn_gate_w': _L0_ffn_in['gate_w'], 'L0_ffn_gate_b': _L0_ffn_in['gate_b'], 'L0_ffn_w1': _L0_ffn_in['w1'], 'L0_ffn_b1': _L0_ffn_in['b1'], 'L0_ffn_w2': _L0_ffn_in['w2'], 'L0_ffn_b2': _L0_ffn_in['b2'], 'L0_ffn_gamma': _L0_ffn_in['gamma'], 'L0_ffn_beta': _L0_ffn_in['beta']}

def reference(x, src, dst, L0_gnn_W, L0_gnn_a_src, L0_gnn_a_dst, L0_ffn_gate_w, L0_ffn_gate_b, L0_ffn_w1, L0_ffn_b1, L0_ffn_w2, L0_ffn_b2, L0_ffn_gamma, L0_ffn_beta):
    import jax
    import jax.numpy as jnp

    def _L0_gnn_ref(x, edge_index, W, a_src, a_dst):
        import jax, jax.numpy as jnp
        import numpy as np
        N = 6250
        E = 100000
        H, F_IN, F_OUT = (8, 256, 32)
        src, dst = (edge_index[0], edge_index[1])
        h = jnp.einsum('ni,hio->hno', x, W)
        attn_src = jnp.einsum('hno,ho->hn', h, a_src[..., 0])
        attn_dst = jnp.einsum('hno,ho->hn', h, a_dst[..., 0])
        edge_attn = jax.nn.leaky_relu(attn_src[:, src] + attn_dst[:, dst], negative_slope=0.2)
        edge_attn_exp = jnp.exp(edge_attn - jnp.max(edge_attn))
        attn_sum = jax.ops.segment_sum(edge_attn_exp.T, dst, num_segments=N)
        attn_norm = edge_attn_exp / (attn_sum[dst].T + 1e-10)
        weighted_h = attn_norm[..., None] * h[:, src]
        out = jax.ops.segment_sum(weighted_h.transpose(1, 0, 2), dst, num_segments=N)
        out = out.reshape(N, H * F_OUT)
        return out + x

    def _L0_ffn_ref(x, gate_w, gate_b, w1, b1, w2, b2, gamma, beta):
        import jax, jax.numpy as jnp
        import numpy as np
        B, S, H, F, E, K = (8, 256, 256, 512, 16, 2)
        EPS = 1e-05
        gate_logits = x @ gate_w + gate_b
        topk_vals, topk_idx = jax.lax.top_k(gate_logits, K)
        topk_w = jax.nn.softmax(topk_vals, axis=-1)
        h = jax.nn.relu(jnp.einsum('bsh,ehf->bsef', x, w1) + b1)
        expert_out = jnp.einsum('bsef,efh->bseh', h, w2) + b2
        sel = jnp.take_along_axis(expert_out, topk_idx[:, :, :, None], axis=2)
        moe = jnp.sum(topk_w[..., None] * sel, axis=2)
        y = x + moe
        mu = jnp.mean(y, axis=-1, keepdims=True)
        var = jnp.var(y, axis=-1, keepdims=True)
        return (y - mu) / jnp.sqrt(var + EPS) * gamma + beta
    edge_index = jnp.stack([src, dst])
    x = x + _L0_gnn_ref(_layernorm(x, axis=-1), edge_index, L0_gnn_W, L0_gnn_a_src, L0_gnn_a_dst)
    x = x + _L0_ffn_ref(_layernorm(x, axis=-1)[None], L0_ffn_gate_w, L0_ffn_gate_b, L0_ffn_w1, L0_ffn_b1, L0_ffn_w2, L0_ffn_b2, L0_ffn_gamma, L0_ffn_beta)[0]
    return x

_drawn_inputs = setup_inputs


def setup_inputs(seed=0):
    import zlib

    import numpy as np

    out = dict(_drawn_inputs(seed))
    spreads = {'L0_ffn_gate_b': (0.0, 0.348),
     'L0_ffn_b1': (0.0, 0.8),
     'L0_ffn_b2': (0.0, 0.328),
     'L0_ffn_gamma': (1.0, 0.2),
     'L0_ffn_beta': (0.0, 0.1)}
    factors = {'L0_ffn_w1': 2.763}
    for name, (base, spread) in spreads.items():
        noise = np.random.default_rng([zlib.crc32(name.encode()), seed]).standard_normal(out[name].shape)
        drawn = base * np.exp(spread * noise) if base else spread * noise
        out[name] = jnp.asarray(drawn.astype(out[name].dtype))
    for name, factor in factors.items():
        out[name] = (out[name] * factor).astype(out[name].dtype)
    return out
```

```python
from contextlib import ExitStack

import concourse.bass as bass
from concourse import mybir
from concourse.alu_op_type import AluOpType as ALU

ACT = mybir.ActivationFunctionType
AXIS_FREE = mybir.AxisListType.X
F32 = mybir.dt.float32
I32 = mybir.dt.int32
U32 = mybir.dt.uint32

P = 128
NODES = 6250
EDGES = 100000
HEADS, F_IN, F_OUT = 8, 256, 32
EXPERTS, HIDDEN, TOP_K = 16, 512, 2
LN_EPS = 1e-5
SUM_EPS = 1e-10
SLOPE = 0.2
FAR_BELOW = -1e30
EXP_TOP = 80.0

TILES = -(-NODES // P)
LAST_ROWS = NODES - (TILES - 1) * P
CHUNKS = -(-EDGES // P)
GROUP = 8
GROUPS = -(-(CHUNKS + TILES - 1) // GROUP)
STEPS = GROUPS * GROUP
STEP_BLOCKS = -(-STEPS // P)
ROW = F_IN + HEADS
AD = HEADS + 1
BATCH = 7
BATCHES = TILES // BATCH
SLOT_TILES = (NODES * TOP_K + EXPERTS * (P - 1)) // P
BLOCKS = EXPERTS * TILES
NO_ROW = 1 << 20
KC = F_IN // P
FC = HIDDEN // P

assert TILES % BATCH == 0 and SLOT_TILES <= P and ROW <= 512


class Marks:

    def __init__(self):
        self.at = {}

    def put(self, name, sem, value):
        assert name not in self.at, name
        self.at[name] = (sem, value)


class Queue:

    def __init__(self, marks, sem):
        self.marks, self.sem, self.count, self.items = marks, sem, 0, []

    def do(self, emit, name=None):
        if name is not None:
            self.count += 1
            self.marks.put(name, self.sem, self.count)
        self.items.append(("do", emit, self.sem if name is not None else None))

    def dma(self, emit, counter, name):
        counter[1] += 16
        if name is not None:
            self.marks.put(name, counter[0], counter[1])
        self.items.append(("dma", emit, counter[0]))

    def wait(self, *names):
        for name in names:
            self.items.append(("wait", name, None))

    def emit(self, eng):
        passed = {}
        for kind, what, sem in self.items:
            if kind == "wait":
                s, value = self.marks.at[what]
                if passed.get(s.name, 0) < value:
                    eng.wait_ge(s, value)
                    passed[s.name] = value
            else:
                ins = what(eng)
                if sem is not None:
                    ins.then_inc(sem, 16 if kind == "dma" else 1)


def build_program(nc, x, src, dst, w_gnn, a_src, a_dst, gate_w, gate_b, w1, b1, w2, b2, gamma, beta, out):
    ctx = ExitStack()
    with ctx:
        ctx.enter_context(nc.allow_non_contiguous_dma(reason="one dst per chunk, few and small"))

        def sb(name, shape, dt=F32):
            return ctx.enter_context(nc.sbuf_tensor(name, shape, dt))

        def dram(name, shape, dt=F32):
            return nc.dram_tensor(name, shape, dt, kind="Internal").ap()

        def sem(name):
            return ctx.enter_context(nc.semaphore(name))

        def counter(name):
            return [sem(name), 0]

        node_rows = dram("node_rows", [TILES * P, ROW])
        x_plus_xn = dram("x_plus_xn", [TILES * P, F_IN])
        x1_beta = dram("x1_beta", [TILES * P, F_IN])
        y0_rows = dram("y0_rows", [TILES * P, F_IN])
        choice_rows = dram("choice_rows", [TILES * P * TOP_K, F_IN])
        src_pad = dram("src_pad", [CHUNKS * P], I32)
        dst_pad = dram("dst_pad", [CHUNKS * P], I32)
        slot_table = dram("slot_table", [(BLOCKS + 1) * P, 1], I32)

        region0 = sb("region0", [P, EXPERTS * KC * HIDDEN])
        region1 = sb("region1", [P, EXPERTS * FC * F_IN])
        region2 = sb("region2", [P, 7 * 1024 + 512])
        region3 = sb("region3", [P, 2 * STEPS + 24 * P])
        x_all = region0[:, 0:TILES * F_IN].rearrange("p (t f) -> p t f", f=F_IN)
        w1_sb = region0[:, :]
        w2_sb = region1[:, :]
        acc = region1[:, 0:TILES * ROW]
        acc_t = acc.rearrange("p (t c) -> p t c", c=ROW)
        over_chunks = region1[:, 0:10 * CHUNKS].rearrange("p (n c) -> p n c", c=CHUNKS)
        first_bc, delta_bc, iota_chunk, junk = [over_chunks[:, n, :] for n in range(4)]
        row_a, row_b, row_c, row_d = [over_chunks[0:1, n, :] for n in range(4, 8)]
        ends_i = over_chunks[0:1, 8:10, :].bitcast(I32)
        blank = region1[0:BLOCKS // BATCH, 10 * CHUNKS:10 * CHUNKS + BATCH * P].bitcast(I32)
        behind = TILES * ROW

        def next_behind(parts, width):
            nonlocal behind
            behind += width
            return region1[0:parts, behind - width:behind]
        rows_i = next_behind(P, 4 * P).rearrange("p (s m) -> p s m", m=P).bitcast(I32)
        rows_f = next_behind(P, 4 * P).rearrange("p (s m) -> p s m", m=P)
        w_cat = next_behind(P, KC * (ROW + HEADS)).rearrange("p (c m) -> p c m", c=KC)
        a_bc = next_behind(P, 2 * F_IN).rearrange("p (n f) -> p n f", n=2)
        b1_rows = next_behind(EXPERTS, HIDDEN)
        pad_i = next_behind(1, 2 * P).bitcast(I32)
        assert behind <= EXPERTS * FC * F_IN
        dloc = region3[:, 0:STEPS]
        src_idx = region3[:, STEPS:2 * STEPS].bitcast(U32)
        oh_base = 2 * STEPS
        onehot = region3[:, oh_base:oh_base + 24 * P].rearrange("p (s m) -> p s m", m=P)
        onehot_t = region1[:, TILES * ROW:TILES * ROW + 8 * P].rearrange("p (s m) -> p s m", m=P)
        b2_bc = region3[:, 0:EXPERTS * F_IN]
        cut = [0, TILES * EXPERTS, TILES * 8, TILES * 8, (TILES + 1) * EXPERTS]
        logits, top_v, top_i, base = [
            region3[:, sum(cut[:n + 1]):sum(cut[:n + 2])].rearrange("p (t e) -> p t e", e=e)
            for n, e in enumerate((EXPERTS, 8, 8, EXPERTS))]
        top_i = top_i.bitcast(U32)

        iota_row_i = sb("iota_row_i", [P, P], I32)
        iota_row = sb("iota_row", [P, P])
        iota_col_i = sb("iota_col_i", [P, 1], I32)
        iota_col = sb("iota_col", [P, 1])
        ident = sb("ident", [P, P])
        before = sb("before", [P, P])
        ones = sb("ones", [P, P])
        kcol_i = sb("kcol_i", [P, STEP_BLOCKS], I32)
        kcol = sb("kcol", [P, STEP_BLOCKS])
        step_c = sb("step_c", [P, STEP_BLOCKS])
        step_ci = sb("step_ci", [P, STEP_BLOCKS], U32)
        step_d = sb("step_d", [P, STEP_BLOCKS])
        step_t = sb("step_t", [P, STEP_BLOCKS])
        step_t128 = sb("step_t128", [P, STEP_BLOCKS])
        step_tc = sb("step_tc", [P, STEP_BLOCKS])
        tile_row = sb("tile_row", [1, STEP_BLOCKS * P], I32)
        tfirst = sb("tfirst", [1, GROUPS])
        tile_base = sb("tile_base", [P, TILES, AD])
        stats = sb("stats", [P, BATCH, 6])
        mean_var = sb("mean_var", [P, TILES, 2])
        var_eps = sb("var_eps", [P, TILES])
        std = sb("std", [P, TILES])
        rstd = sb("rstd", [P, TILES])
        shift = sb("shift", [P, TILES])
        neg_max = sb("neg_max", [P, GROUPS + 1])
        run_max = sb("run_max", [1, GROUPS + 1])
        fall = sb("fall", [P, GROUPS])
        z = sb("z", [P, 2, GROUP, HEADS])
        cap = sb("cap", [P, 2, GROUP])
        zmax = sb("zmax", [P, 2])
        gmax = sb("gmax", [1, 2])
        late = sb("late", [P, GROUPS])
        late_min = sb("late_min", [P, 1])
        eps_row = sb("eps_row", [1, P])
        eps_bc = sb("eps_bc", [P, TILES])
        rsum = sb("rsum", [P, TILES, HEADS])
        gate_sb = sb("gate_sb", [P, KC, EXPERTS])
        gate_b_sb = sb("gate_b_sb", [1, EXPERTS])
        top_f = sb("top_f", [P, BATCH, TOP_K])
        chosen = sb("chosen", [P, TOP_K, BATCH, EXPERTS])
        both = sb("both", [P, BATCH, EXPERTS])
        rank = sb("rank", [P, BATCH, EXPERTS])
        picked = sb("picked", [P, TOP_K, BATCH, EXPERTS])
        pos_f = sb("pos_f", [P, TOP_K, BATCH])
        pos_i = sb("pos_i", [P, TOP_K, TILES], U32)
        dest_i = sb("dest_i", [P, TILES, TOP_K], I32)
        row_ok = sb("row_ok", [P, 1])
        weight = sb("weight", [P, TOP_K, TILES])
        gap = sb("gap", [P, TILES])
        cnt_f = sb("cnt_f", [P, EXPERTS])
        cnt_i = sb("cnt_i", [P, EXPERTS], I32)
        ntile = sb("ntile", [P, EXPERTS])
        incl = sb("incl", [P, EXPERTS])
        excl = sb("excl", [P, EXPERTS])
        small = sb("small", [P, 6])
        smalls = sb("smalls", [P, EXPERTS])
        blk_i = sb("blk_i", [P, 1], U32)
        expert_row = sb("expert_row", [1, P], I32)
        slots_i = sb("slots_i", [P, P], I32)
        slots_f = sb("slots_f", [P, P])
        dest_u = sb("dest_u", [P, P], U32)
        token_u = sb("token_u", [P, P], U32)
        b1_col = sb("b1_col", [P, FC, EXPERTS])
        gamma_bc = sb("gamma_bc", [P, F_IN])
        beta_bc = sb("beta_bc", [P, F_IN])

        bank = [ctx.enter_context(nc.psum_tensor(f"bank{i}", [P, 512], F32)) for i in range(8)]

        marks = Marks()
        V = Queue(marks, sem("vector_done"))
        S = Queue(marks, sem("scalar_done"))
        T = Queue(marks, sem("tensor_done"))
        G = Queue(marks, sem("pool_done"))
        D = Queue(marks, sem("sync_done"))

        def copy_s(out_, in_):
            return lambda e: e.activation(out_, in_, ACT.Copy)

        ld = {n: counter(f"ld_{n}") for n in ("dstcopy", "srccopy", "ends", "wg", "gate", "b1")}
        D.dma(lambda e: e.dma_start(dst_pad[0:EDGES].rearrange("(a b) -> a b", a=16),
                                    dst.rearrange("(a b) -> a b", a=16)), ld["dstcopy"], None)
        D.dma(lambda e: e.dma_start(src_pad[0:EDGES].rearrange("(a b) -> a b", a=16),
                                    src.rearrange("(a b) -> a b", a=16)), ld["srccopy"], None)
        D.dma(lambda e: e.dma_start(ends_i[:, 0, :], dst.rearrange("(a n) -> a n", a=1)[:, 0:EDGES:P]),
              ld["ends"], None)
        D.dma(lambda e: e.dma_start(ends_i[:, 1, 0:CHUNKS - 1],
                                    dst.rearrange("(a n) -> a n", a=1)[:, P - 1:EDGES:P]), ld["ends"], None)
        D.dma(lambda e: e.dma_start(ends_i[:, 1, CHUNKS - 1:CHUNKS],
                                    dst.rearrange("(a n) -> a n", a=1)[:, EDGES - 1:EDGES]), ld["ends"], "ends")
        for c in range(KC):
            D.dma(lambda e, c=c: e.dma_start(w_cat[:, c, 0:F_IN].rearrange("p (h o) -> p h o", o=F_OUT),
                                             w_gnn[:, c * P:(c + 1) * P, :].rearrange("h p o -> p h o")),
                  ld["wg"], None)
        for n, a in enumerate((a_src, a_dst)):
            D.dma(lambda e, n=n, a=a: e.dma_start(
                a_bc[:, n, :], a.rearrange("h o x -> (x h o)").partition_broadcast(P)), ld["wg"], "wg" if n == 1 else None)
        xl = [counter(f"ld_x{q}") for q in range(BATCHES)]
        V.do(lambda e: e.memset(x_all[:, TILES - 1, :], 0.0), "x_tail")
        for q in range(BATCHES):
            full = BATCH if q < BATCHES - 1 else BATCH - 1
            r0 = q * BATCH * P
            D.dma(lambda e, q=q, full=full, r0=r0: e.dma_start(
                x_all[:, q * BATCH:q * BATCH + full, :],
                x[r0:r0 + full * P, :].rearrange("(t p) f -> p t f", p=P)), xl[q],
                ("x", q) if full == BATCH else None)
        D.wait("x_tail")
        D.dma(lambda e: e.dma_start(x_all[0:LAST_ROWS, TILES - 1, :], x[(TILES - 1) * P:NODES, :]),
              xl[BATCHES - 1], ("x", BATCHES - 1))

        G.do(lambda e: e.memset(pad_i[:, 0:P], 0), None)
        G.do(lambda e: e.memset(pad_i[:, P:2 * P], -1), "pad")
        G.do(lambda e: e.iota(iota_row_i[:, :], [[1, P]], base=0, channel_multiplier=0))
        G.do(lambda e: e.iota(iota_col_i[:, :], [[0, 1]], base=0, channel_multiplier=1))
        G.do(lambda e: e.iota(kcol_i[:, :], [[P, STEP_BLOCKS]], base=0, channel_multiplier=1))
        G.do(lambda e: e.iota(junk.bitcast(I32), [[1, CHUNKS]], base=0, channel_multiplier=0), "iotas")
        G.do(lambda e: e.memset(blank[:, :], NO_ROW), "blank")
        G.do(lambda e: e.iota(dest_i[:, :, :], [[2 * P, TILES], [1, TOP_K]], base=0, channel_multiplier=2),
             "dest")

        S.wait("pad")
        tail = CHUNKS * P - EDGES
        S.dma(lambda e: e.dma_start(src_pad[EDGES:].rearrange("(a n) -> a n", a=1), pad_i[:, 0:tail]),
              ld["srccopy"], "src_pad")
        S.dma(lambda e: e.dma_start(dst_pad[EDGES:].rearrange("(a n) -> a n", a=1), pad_i[:, P:P + tail]),
              ld["dstcopy"], "dst_pad")
        S.dma(lambda e: e.dma_start(gate_sb[:, :, :], gate_w.rearrange("(c p) e -> p c e", p=P)),
              ld["gate"], None)
        S.dma(lambda e: e.dma_start(gate_b_sb[:, :], gate_b.rearrange("(a n) -> a n", a=1)), ld["gate"], "gate")
        S.dma(lambda e: e.dma_start(b1_rows[:, :], b1), ld["b1"], None)
        S.dma(lambda e: e.dma_start(gamma_bc[:, :], gamma.partition_broadcast(P)), ld["b1"], None)
        S.dma(lambda e: e.dma_start(beta_bc[:, :], beta.partition_broadcast(P)), ld["b1"], "b1")
        tb = counter("blank_dma")
        S.wait("blank")
        S.dma(lambda e: e.dma_start(
            slot_table[0:BLOCKS * P, :].rearrange("(p n) o -> p (n o)", n=BATCH * P), blank[:, :]), tb, None)
        S.dma(lambda e: e.dma_start(
            slot_table[BLOCKS * P:, :].rearrange("(a n) o -> a (n o)", a=1), blank[0:1, 0:P]), tb, "table0")

        V.wait("iotas")
        V.do(lambda e: e.tensor_copy(iota_row[:, :], iota_row_i[:, :]))
        V.do(lambda e: e.tensor_copy(iota_col[:, :], iota_col_i[:, :]))
        V.do(lambda e: e.tensor_copy(kcol[:, :], kcol_i[:, :]))
        V.do(lambda e: e.tensor_copy(iota_chunk, junk.bitcast(I32)), "iota_f")
        V.wait("iota_f")
        V.do(lambda e: e.tensor_scalar(ident[:, :], iota_row[:, :], iota_col[:, :], None, ALU.is_equal))
        V.do(lambda e: e.tensor_scalar(before[:, :], iota_row[:, :], iota_col[:, :], None, ALU.is_gt))
        V.do(lambda e: e.memset(ones[:, :], 1.0), "consts")
        V.do(lambda e: e.tensor_scalar(row_ok[:, :], iota_col[:, :], float(LAST_ROWS), None, ALU.is_lt))
        V.do(lambda e: e.memset(tile_base[:, :, HEADS:AD], 1.0))
        V.do(lambda e: e.memset(neg_max[:, 0:1], -FAR_BELOW))
        V.do(lambda e: e.memset(run_max[:, 0:1], FAR_BELOW), "inits")

        V.wait("ends")
        V.do(lambda e: e.tensor_scalar(ends_i[:, :, :], ends_i[:, :, :], 7, None, ALU.arith_shift_right), "t0")
        V.wait("t0")
        V.do(lambda e: e.tensor_copy(row_a[:, :], ends_i[:, 0, :]))
        V.do(lambda e: e.tensor_copy(row_b[:, :], ends_i[:, 1, :]))
        V.do(lambda e: e.memset(row_d[:, :], 1.0), "t1")
        V.wait("t1")
        V.do(lambda e: e.scalar_tensor_tensor(row_b[:, :], row_b[:, :], 1.0, row_a[:, :], ALU.add,
                                              ALU.subtract), "t2")
        V.wait("t2")
        V.do(lambda e: e.tensor_tensor_scan(row_c[:, :], row_d[:, :], row_b[:, :], 0.0, ALU.mult, ALU.add),
             "t3")
        V.wait("t3")
        V.do(lambda e: e.tensor_tensor(row_c[:, :], row_c[:, :], row_b[:, :], ALU.subtract), "t4")
        V.wait("t4")
        V.do(lambda e: e.tensor_tensor(row_d[:, :], row_a[:, :], row_c[:, :], ALU.subtract), "t5")
        T.wait("consts", "t5")
        for n, row in enumerate((row_c, row_d)):
            for b in range(2):
                lo, hi = b * 512, min(CHUNKS, b * 512 + 512)
                T.do(lambda e, n=n, b=b, row=row, lo=lo, hi=hi: e.matmul(
                    bank[2 * n + b][:, 0:hi - lo], ones[0:1, :], row[:, lo:hi], start=True, stop=True),
                    ("chunk_bc", n, b))
        for n, to in enumerate((first_bc, delta_bc)):
            for b in range(2):
                lo, hi = b * 512, min(CHUNKS, b * 512 + 512)
                S.wait(("chunk_bc", n, b))
                S.do(copy_s(to[:, lo:hi], bank[2 * n + b][:, 0:hi - lo]), ("chunk_sb", n, b))
        V.wait(("chunk_sb", 1, 1))
        for b in range(STEP_BLOCKS):
            V.do(lambda e, b=b: e.tensor_scalar(junk, first_bc, kcol[:, b:b + 1], 0.0, ALU.is_le, ALU.add,
                                                accum_out=step_c[:, b:b + 1]), ("count", b))
            V.wait(("count", b))
        V.do(lambda e: e.tensor_scalar(step_c[:, :], step_c[:, :], -1.0, None, ALU.add), "step_c")
        V.wait("step_c")
        V.do(lambda e: e.tensor_copy(step_ci[:, :], step_c[:, :]), "step_ci")
        for b in range(STEP_BLOCKS):
            V.do(lambda e, b=b: e.scalar_tensor_tensor(junk, iota_chunk, step_c[:, b:b + 1], delta_bc,
                                                       ALU.is_equal, ALU.mult,
                                                       accum_out=step_d[:, b:b + 1]), ("delta", b))
            V.wait(("delta", b))
        V.do(lambda e: e.tensor_tensor(step_t[:, :], step_d[:, :], kcol[:, :], ALU.add), "step_t")
        V.wait("step_t")
        V.do(lambda e: e.tensor_scalar(step_t128[:, :], step_t[:, :], float(P), None, ALU.mult))
        V.do(lambda e: e.tensor_scalar(step_tc[:, :], step_t[:, :], float(TILES - 1), None, ALU.min), "step_tc")
        T.wait("step_tc", ("chunk_sb", 1, 1))
        for n, col in enumerate((step_tc, step_t)):
            for b in range(STEP_BLOCKS):
                T.do(lambda e, n=n, b=b, col=col: e.transpose(
                    bank[2 * n + b // 4][0:1, (b % 4) * P:(b % 4 + 1) * P], col[:, b:b + 1], ident[:, :]),
                    ("tile_tr", n, b))
        V.wait(("tile_tr", 0, STEP_BLOCKS - 1))
        V.do(lambda e: e.tensor_copy(tile_row[:, 0:512], bank[0][0:1, :]))
        V.do(lambda e: e.tensor_copy(tile_row[:, 512:STEP_BLOCKS * P], bank[1][0:1, 0:STEP_BLOCKS * P - 512]),
             "tile_row")
        V.wait(("tile_tr", 1, STEP_BLOCKS - 1))
        half = 512 // GROUP
        V.do(lambda e: e.tensor_copy(tfirst[:, 0:half], bank[2][0:1, 0:512:GROUP]))
        V.do(lambda e: e.tensor_copy(tfirst[:, half:GROUPS], bank[3][0:1, 0:(GROUPS - half) * GROUP:GROUP]),
             "tfirst")
        rows_d = [counter(f"rows_dma{i}") for i in range(4)]
        for b in range(STEP_BLOCKS):
            if b == 0:
                G.wait("step_ci", "src_pad", "dst_pad")
            for n, table in enumerate((src_pad, dst_pad)):
                slot = 2 * (b % 2) + n
                if b >= 2:
                    G.wait(("rows_f", b - 2, n))
                G.dma(lambda e, b=b, slot=slot, table=table: e.indirect_dma_start(
                    rows_i[:, slot, :], None, table.rearrange("(c e) -> c e", e=P),
                    bass.IndirectOffsetOnAxis(step_ci[:, b:b + 1], 0)), rows_d[slot], ("rows", b, n))
        G.wait(("delta", STEP_BLOCKS - 1), "tfirst", ("chunk_bc", 1, 1), "table0")
        G.do(lambda e: e.memset(acc, 0.0), "acc0")
        for b in range(STEP_BLOCKS):
            for n in range(2):
                slot = 2 * (b % 2) + n
                V.wait(("rows", b, n))
                if b >= 2:
                    V.wait(("rows_tr", b - 2, n))
                if n == 0:
                    V.do(lambda e, slot=slot: e.tensor_copy(rows_f[:, slot, :], rows_i[:, slot, :]),
                         ("rows_f", b, n))
                else:
                    V.do(lambda e, slot=slot, b=b: e.tensor_scalar(
                        rows_f[:, slot, :], rows_i[:, slot, :], step_t128[:, b:b + 1], None, ALU.subtract),
                        ("rows_f", b, n))
                T.wait(("rows_f", b, n))
                if b >= 2:
                    T.wait(("rows_sb", b - 2, n))
                elif b == 0:
                    T.wait("tfirst")
                T.do(lambda e, slot=slot: e.transpose(bank[slot][:, 0:P], rows_f[:, slot, :], ident[:, :]),
                     ("rows_tr", b, n))
                w = min(P, STEPS - b * P)
                to = (src_idx, dloc)[n][:, b * P:b * P + w]
                S.wait(("rows_tr", b, n))
                S.do(copy_s(to, bank[slot][:, 0:w]), ("rows_sb", b, n))

        tmp_a = region2[:, 7 * 1024:7 * 1024 + F_IN]
        for c in range(KC):
            for n in range(2):
                V.wait("wg")
                V.do(lambda e, c=c, n=n: e.tensor_tensor(tmp_a, w_cat[:, c, 0:F_IN], a_bc[:, n, :], ALU.mult),
                     ("wa", c, n))
                V.wait(("wa", c, n))
                V.do(lambda e, c=c, n=n: e.tensor_reduce(
                    w_cat[:, c, F_IN + HEADS * n:F_IN + HEADS * (n + 1)],
                    tmp_a.rearrange("p (h o) -> p h o", o=F_OUT), AXIS_FREE, ALU.add), ("w_cat", c, n))
                V.wait(("w_cat", c, n))
        xn_buf = region2[:, 0:1024].rearrange("p (s f) -> p s f", f=F_IN)
        xt_buf = region2[:, 1024:2048].rearrange("p (s f) -> p s f", f=F_IN)
        s_buf = region2[:, 2048:3072].rearrange("p (s f) -> p s f", f=F_IN)
        h_buf = region2[:, 3072:3072 + 8 * ROW].rearrange("p (s c) -> p s c", c=ROW)
        h_out = [counter(f"h_out{i}") for i in range(2)]
        s_out = [counter(f"s_out{i}") for i in range(4)]

        def var_std(tag, t0, n):
            V.wait((tag, "aggr", t0 + n - 1))
            V.do(lambda e: e.tensor_scalar(var_eps[:, t0:t0 + n], mean_var[:, t0:t0 + n, 1], LN_EPS, None,
                                           ALU.add), (tag, "var_eps", t0))
            S.wait((tag, "var_eps", t0))
            S.do(lambda e: e.activation(std[:, t0:t0 + n], var_eps[:, t0:t0 + n], ACT.Sqrt), (tag, "std", t0))

        def inv_std(tag, t0, n):
            V.wait((tag, "std", t0))
            V.do(lambda e: e.reciprocal(rstd[:, t0:t0 + n], std[:, t0:t0 + n]), (tag, "rstd", t0))

        def rstd_of(tag, t0, n):
            var_std(tag, t0, n)
            inv_std(tag, t0, n)

        def stats_of(tag, t, tile_ap):
            k = t % BATCH
            V.do(lambda e: e.bn_stats(stats[:, k, :], tile_ap), (tag, "stats", t))
            V.wait((tag, "stats", t))
            V.do(lambda e: e.bn_aggr(mean_var[:, t, :], stats[:, k, :]), (tag, "aggr", t))

        def many_stats(tag, t0, tile_ap):
            for t in range(t0, t0 + BATCH + 1):
                if t < t0 + BATCH:
                    V.do(lambda e, t=t: e.bn_stats(stats[:, t % BATCH, :], tile_ap(t)), (tag, "stats", t))
                if t > t0:
                    V.wait((tag, "stats", t - 1))
                    V.do(lambda e, t=t: e.bn_aggr(mean_var[:, t - 1, :], stats[:, (t - 1) % BATCH, :]),
                         (tag, "aggr", t - 1))

        H_GROUP = 4
        def a_stats(q):
            V.wait(("x", q))
            many_stats("A", q * BATCH, lambda t: x_all[:, t, :])
            rstd_of("A", q * BATCH, BATCH)

        a_stats(0)
        T.wait(("w_cat", KC - 1, 1))
        for t in range(TILES):
            q, s4 = t // BATCH, t % 4
            if t % BATCH == 3 and q + 1 < BATCHES:
                a_stats(q + 1)
            if t >= 4:
                V.wait(("A_tr", t - 4), ("A_s", t - 4))
            V.wait(("A", "rstd", q * BATCH))
            V.do(lambda e, t=t, s4=s4: e.tensor_scalar(
                xn_buf[:, s4, :], x_all[:, t, :], mean_var[:, t, 0:1], rstd[:, t:t + 1], ALU.subtract,
                ALU.mult), ("A_xn", t))
            G.wait(("A_xn", t))
            if t >= 4:
                G.wait(("s_out", t - 4))
            G.do(lambda e, t=t, s4=s4: e.tensor_tensor(s_buf[:, s4, :], x_all[:, t, :], xn_buf[:, s4, :],
                                                       ALU.add), ("A_s", t))
            D.wait(("A_s", t))
            D.dma(lambda e, t=t, s4=s4: e.dma_start(x_plus_xn[t * P:(t + 1) * P, :], s_buf[:, s4, :]),
                  s_out[s4], ("s_out", t))
            T.wait(("A_xn", t))
            if t == 0:
                T.wait(("rows_sb", STEP_BLOCKS - 1, 1))
            if t >= 2:
                T.wait(("A_xt", t - 2))
            for c in range(KC):
                T.do(lambda e, t=t, c=c, s4=s4: e.transpose(
                    bank[t % 2][:, c * P:(c + 1) * P], xn_buf[:, s4, c * P:(c + 1) * P], ident[:, :]),
                    ("A_tr", t) if c == KC - 1 else None)
            S.wait(("A_tr", t))
            if t >= 4:
                S.wait(("A_mm", t - 4))
            S.do(copy_s(xt_buf[:, s4, :], bank[t % 2][:, 0:F_IN]), ("A_xt", t))

            def a_matmul(t):
                s4 = t % 4
                T.wait(("A_xt", t))
                if t >= 2:
                    T.wait(("A_h", t - 2), ("A_ad", t - 2))
                for c in range(KC):
                    T.do(lambda e, t=t, c=c, s4=s4: e.matmul(
                        bank[2 + t % 2][:, 0:ROW + HEADS], xt_buf[:, s4, c * P:(c + 1) * P], w_cat[:, c, :],
                        start=(c == 0), stop=(c == KC - 1)), ("A_mm", t) if c == KC - 1 else None)
                s8 = t % 8
                S.wait(("A_mm", t))
                if t >= 8 and t % H_GROUP == 0:
                    S.wait(("h_out", t // H_GROUP - 2))
                S.do(copy_s(h_buf[:, s8, :], bank[2 + t % 2][:, 0:ROW]), ("A_h", t))
                S.do(copy_s(tile_base[:, t, 0:HEADS], bank[2 + t % 2][:, ROW:ROW + HEADS]), ("A_ad", t))
                if t % H_GROUP == H_GROUP - 1 or t == TILES - 1:
                    g = t // H_GROUP
                    n = t % H_GROUP + 1
                    D.wait(("A_h", t))
                    D.dma(lambda e, g=g, n=n: e.dma_start(
                        node_rows[g * H_GROUP * P:(g * H_GROUP + n) * P, :].rearrange("(t p) c -> p t c", p=P),
                        h_buf[:, (g % 2) * H_GROUP:(g % 2) * H_GROUP + n, :]), h_out[g % 2], ("h_out", g))
            if t >= 1:
                a_matmul(t - 1)
        a_matmul(TILES - 1)
        H_OUTS = (TILES - 1) // H_GROUP + 1

        T.wait("b1", ("A_h", TILES - 1), ("A_ad", TILES - 1))
        for f in range(FC):
            T.do(lambda e, f=f: e.transpose(bank[7][:, f * EXPERTS:(f + 1) * EXPERTS],
                                            b1_rows[:, f * P:(f + 1) * P], ident[0:EXPERTS, 0:EXPERTS]),
                 ("b1_tr", f))
        S.wait(("b1_tr", FC - 1))
        S.do(copy_s(b1_col[:, :, :].rearrange("p c e -> p (c e)"), bank[7][:, 0:FC * EXPERTS]), "b1_col")

        w1_ld = counter("ld_w1")
        D.wait(("A_xn", TILES - 1), ("A_s", TILES - 1))
        for e0 in range(0, EXPERTS, 4):
            for c in range(KC):
                D.dma(lambda e, e0=e0, c=c: e.dma_start(
                    w1_sb.rearrange("p (x c f) -> p x c f", c=KC, f=HIDDEN)[:, e0:e0 + 4, c, :],
                    w1[e0:e0 + 4, c * P:(c + 1) * P, :].rearrange("x p f -> p x f")), w1_ld,
                    "w1" if e0 + 4 == EXPERTS and c == KC - 1 else None)

        slot_at = [region2[:, i * GROUP * ROW:(i + 1) * GROUP * ROW] for i in range(3)]
        fourth = TILES * ROW + 8 * P
        slot_at.append(region1[:, fourth:fourth + GROUP * ROW])
        gathered = [v.rearrange("p (j c) -> p j c", c=ROW) for v in slot_at]
        SLOTS = len(gathered)
        row_in = [counter(f"row_in{i}") for i in range(SLOTS)]
        for g in range(GROUPS):
            if g == 0:
                for i in (H_OUTS - 2, H_OUTS - 1):
                    G.wait(("h_out", i))
                G.wait(("rows_sb", STEP_BLOCKS - 1, 0))
                for t in range(TILES - 4, TILES):
                    G.wait(("s_out", t))
                G.wait(("A_mm", TILES - 1))
            if g == SLOTS - 1:
                G.wait("b1_col")
            if g >= SLOTS:
                G.wait(("agg", g - SLOTS, GROUP - 1))
            for j in range(GROUP):
                k = g * GROUP + j
                G.dma(lambda e, g=g, j=j, k=k: e.indirect_dma_start(
                    gathered[g % SLOTS][:, j, :], None, node_rows,
                    bass.IndirectOffsetOnAxis(src_idx[:, k:k + 1], 0)), row_in[g % SLOTS],
                    ("row_in", g) if j == GROUP - 1 else None)

        TR_BANKS, Z_BANKS, M_BANK, AGG_BANKS = (0, 1), (2, 3), 4, (5, 6, 7)

        def b_onehot(g):
            if g == 0:
                V.wait(("rows_sb", STEP_BLOCKS - 1, 1))
            if g >= 3:
                V.wait(("agg", g - 3, GROUP - 1))
            for j in range(GROUP):
                k = g * GROUP + j
                V.do(lambda e, g=g, j=j, k=k: e.tensor_scalar(
                    onehot[:, (g % 3) * GROUP + j, :], iota_row[:, :], dloc[:, k:k + 1], None, ALU.is_equal),
                    ("onehot", g, j) if j % 4 == 3 else None)

        def b_transposes(g):
            for half in range(2):
                T.wait(("onehot", g, half * 4 + 3))
                if g >= 1:
                    T.wait(("oh_t", g - 1, half))
                for j in range(half * 4, half * 4 + 4):
                    T.do(lambda e, g=g, j=j, half=half: e.transpose(
                        bank[TR_BANKS[half]][:, (j % 4) * P:(j % 4 + 1) * P],
                        onehot[:, (g % 3) * GROUP + j, :], ident[:, :]),
                        ("oh_tr", g, half) if j % 4 == 3 else None)
                S.wait(("oh_tr", g, half))
                if g >= 1:
                    S.wait(("ad_mm", g - 1))
                S.do(copy_s(onehot_t[:, half * 4:half * 4 + 4, :].rearrange("p s m -> p (s m)"),
                            bank[TR_BANKS[half]][:, :]), ("oh_t", g, half))

        def b_attn_dst(g):
            T.wait(("oh_t", g, 1))
            if g == 0:
                T.wait("tile_row", "inits", ("A_ad", TILES - 1))
            if g >= 2:
                T.wait(("z_add", g - 2), ("cap", g - 2))

            def emit(e, g=g):
                _, tiles = nc.values_load_multi_w_load_instructions(
                    tile_row[0:1, g * GROUP:(g + 1) * GROUP], engines=[mybir.EngineType.PE], min_val=0,
                    max_val=TILES - 1, skip_runtime_bounds_check_because="the value was clamped on chip")
                flat = tile_base[:, :, :].rearrange("p t c -> p (t c)")
                for j in range(GROUP):
                    ins = e.matmul(bank[Z_BANKS[g % 2]][:, j * AD:(j + 1) * AD], onehot_t[:, j, :],
                                   flat[:, bass.ds(tiles[j] * AD, AD)], start=True, stop=True)
                return ins
            T.do(emit, ("ad_mm", g))
            S.wait(("ad_mm", g))
            if g >= 2:
                S.wait(("z_cap", g - 2))
            S.do(lambda e, g=g: e.activation(
                cap[:, g % 2, :],
                bank[Z_BANKS[g % 2]][:, 0:GROUP * AD].rearrange("p (j c) -> p j c", c=AD)[:, :, HEADS],
                ACT.Copy, bias=FAR_BELOW, scale=-2.0 * FAR_BELOW), ("cap", g))

        def b_logits(g):
            zg = z[:, g % 2, :, :]
            V.wait(("row_in", g), ("cap", g))
            if g >= 2:
                V.wait(("p", g - 2))
            V.do(lambda e: e.tensor_tensor(
                zg, bank[Z_BANKS[g % 2]][:, 0:GROUP * AD].rearrange("p (j c) -> p j c", c=AD)[:, :, 0:HEADS],
                gathered[g % SLOTS][:, :, F_IN:ROW], ALU.add), ("z_add", g))
            V.wait(("z_add", g))
            V.do(lambda e: e.scalar_tensor_tensor(zg, zg, SLOPE, zg, ALU.mult, ALU.max), ("z_relu", g))
            V.wait(("z_relu", g), ("cap", g))
            V.do(lambda e: e.tensor_tensor(zg, zg, cap[:, g % 2, :].unsqueeze(2).broadcast_to(
                [P, GROUP, HEADS]), ALU.min), ("z_cap", g))
            V.wait(("z_cap", g))
            if g >= 2:
                V.wait(("max_tr", g - 2))
            V.do(lambda e: e.tensor_reduce(zmax[:, g % 2:g % 2 + 1], zg.rearrange("p j h -> p (j h)"),
                                           AXIS_FREE, ALU.max), ("zmax", g))

        def b_max_tr(g):
            T.wait(("zmax", g))
            if g >= 1:
                T.wait(("gmax", g - 1))
            T.do(lambda e: e.transpose(bank[M_BANK][0:1, 0:P], zmax[:, g % 2:g % 2 + 1], ident[:, :]),
                 ("max_tr", g))

        def b_max(g):
            V.wait(("max_tr", g))
            V.do(lambda e: e.tensor_reduce(gmax[:, g % 2:g % 2 + 1], bank[M_BANK][0:1, 0:P], AXIS_FREE,
                                           ALU.max), ("gmax", g))
            V.wait(("gmax", g))
            V.do(lambda e: e.tensor_tensor(run_max[:, g + 1:g + 2], run_max[:, g:g + 1],
                                           gmax[:, g % 2:g % 2 + 1], ALU.max), ("run_max", g))

        def b_max_bc(g):
            T.wait(("run_max", g))
            if g >= 1:
                T.wait(("neg_max", g - 1))
            T.do(lambda e: e.matmul(bank[M_BANK][:, P + 8:P + 9], ones[0:1, :], run_max[:, g + 1:g + 2],
                                    start=True, stop=True), ("max_bc", g))

        def b_exp(g):
            S.wait(("max_bc", g))
            S.do(lambda e: e.activation(neg_max[:, g + 1:g + 2], bank[M_BANK][:, P + 8:P + 9], ACT.Copy,
                                        scale=-1.0), ("neg_max", g))
            S.wait(("neg_max", g), ("z_cap", g))
            S.do(lambda e: e.activation(gathered[g % SLOTS][:, :, F_IN:ROW], z[:, g % 2, :, :], ACT.Exp,
                                        bias=neg_max[:, g + 1:g + 2]), ("p", g))
            S.do(lambda e: e.activation(fall[:, g:g + 1], neg_max[:, g:g + 1], ACT.Exp, scale=-1.0,
                                        bias=neg_max[:, g + 1:g + 2]), ("fall", g))

        def b_weigh(g):
            V.wait(("p", g))
            for half in range(2):
                js = slice(half * 4, half * 4 + 4)
                hv = gathered[g % SLOTS][:, js, 0:F_IN].rearrange("p j (h o) -> p j h o", o=F_OUT)
                pv = gathered[g % SLOTS][:, js, F_IN:ROW].unsqueeze(3).broadcast_to([P, 4, HEADS, F_OUT])
                V.do(lambda e, hv=hv, pv=pv: e.tensor_tensor(hv, hv, pv, ALU.mult), ("weigh", g, half))

        def b_aggregate(g, js):
            for j in js:
                k = g * GROUP + j
                T.wait(("weigh", g, j // 4))
                if k >= 3:
                    T.wait(("add", (k - 3) // GROUP, (k - 3) % GROUP))
                T.do(lambda e, g=g, j=j, k=k: e.matmul(
                    bank[AGG_BANKS[k % 3]][:, 0:ROW], onehot[:, (g % 3) * GROUP + j, :],
                    gathered[g % SLOTS][:, j, :], start=True, stop=True), ("agg", g, j))

        add_tiles = {}

        def b_add(g, js):
            def load(e, g=g):
                _, add_tiles[g] = nc.values_load_multi_w_load_instructions(
                    tile_row[0:1, g * GROUP:(g + 1) * GROUP], engines=[mybir.EngineType.DVE], min_val=0,
                    max_val=TILES - 1, skip_runtime_bounds_check_because="the value was clamped on chip")
            if js[0] == 0:
                V.wait(("fall", g))
                if g == 0:
                    V.wait("acc0", "tile_row")
                V.do(load)
            for j in js:
                k = g * GROUP + j
                V.wait(("agg", g, j))
                if k >= 1:
                    V.wait(("add", (k - 1) // GROUP, (k - 1) % GROUP))

                def emit(e, g=g, j=j, k=k):
                    rows = acc[:, bass.ds(add_tiles[g][j] * ROW, ROW)]
                    new = bank[AGG_BANKS[k % 3]][:, 0:ROW]
                    if j == 0:
                        return e.scalar_tensor_tensor(rows, rows, fall[:, g:g + 1], new, ALU.mult, ALU.add)
                    return e.tensor_tensor(rows, rows, new, ALU.add)
                V.do(emit, ("add", g, j))

        b_onehot(0)
        b_transposes(0)
        b_attn_dst(0)
        for g in range(GROUPS + 1):
            if g < GROUPS:
                b_logits(g)
            if g + 1 < GROUPS:
                b_onehot(g + 1)
            if g >= 1:
                b_aggregate(g - 1, range(0, 3))
            if g < GROUPS:
                b_max_tr(g)
            if g + 1 < GROUPS:
                b_transposes(g + 1)
            if g >= 1:
                b_add(g - 1, range(0, 3))
                b_aggregate(g - 1, range(3, 5))
            if g < GROUPS:
                b_max(g)
                b_max_bc(g)
                b_exp(g)
            if g >= 1:
                b_aggregate(g - 1, range(5, GROUP))
                b_add(g - 1, range(3, GROUP))
            if g + 1 < GROUPS:
                b_attn_dst(g + 1)
            if g < GROUPS:
                b_weigh(g)

        LAST = ("add", GROUPS - 1, GROUP - 1)
        T.wait("tfirst", LAST)
        T.do(lambda e: e.matmul(bank[0][:, 0:GROUPS], ones[0:1, :], tfirst[:, :], start=True, stop=True),
             "tfirst_bc")
        V.wait("tfirst_bc", ("neg_max", GROUPS - 1))
        V.do(lambda e: e.tensor_scalar(late[:, :], bank[0][:, 0:GROUPS], iota_col[:, :], -FAR_BELOW,
                                       ALU.is_gt, ALU.mult), "late")
        V.wait("late")
        V.do(lambda e: e.tensor_tensor(late[:, :], late[:, :], neg_max[:, 1:GROUPS + 1], ALU.add), "late2")
        V.wait("late2")
        V.do(lambda e: e.tensor_reduce(late_min[:, :], late[:, :], AXIS_FREE, ALU.min), "late_min")
        V.wait("late_min")
        V.do(lambda e: e.tensor_scalar(late_min[:, :], late_min[:, :], neg_max[:, GROUPS:GROUPS + 1], EXP_TOP,
                                       ALU.subtract, ALU.min), "late3")
        S.wait("late3")
        S.do(lambda e: e.activation(late_min[:, :], late_min[:, :], ACT.Exp), "late4")
        T.wait("late4", "late")
        T.do(lambda e: e.transpose(bank[0][0:1, 0:P], late_min[:, :], ident[:, :]), "eps_tr")
        V.wait("eps_tr")
        V.do(lambda e: e.tensor_scalar(eps_row[:, :], bank[0][0:1, 0:P], SUM_EPS, None, ALU.mult), "eps_row")
        T.wait("eps_row")
        T.do(lambda e: e.matmul(bank[1][:, 0:TILES], ones[0:1, :], eps_row[:, 0:TILES], start=True, stop=True),
             "eps_bc")
        V.wait("eps_bc")
        V.do(lambda e: e.tensor_copy(eps_bc[:, :], bank[1][:, 0:TILES]), "eps")
        V.wait("eps", LAST)
        V.do(lambda e: e.tensor_tensor(rsum[:, :, :], acc_t[:, :, F_IN:ROW],
                                       eps_bc[:, :].unsqueeze(2).broadcast_to([P, TILES, HEADS]), ALU.add),
             "sums")
        V.wait("sums")
        V.do(lambda e: e.reciprocal(rsum[:, :, :], rsum[:, :, :]), "rsum")
        V.do(lambda e: e.tensor_scalar(base[:, 0, :], iota_row[:, 0:EXPERTS], float(TILES * P), None, ALU.mult),
             "base0")

        s_all = region2[:, 0:2 * BATCH * F_IN].rearrange("p (s t f) -> p s t f", s=2, f=F_IN)
        y_all = region2[:, 2 * BATCH * F_IN:4 * BATCH * F_IN].rearrange("p (s t f) -> p s t f", s=2, f=F_IN)
        yt_buf = region2[:, 4 * BATCH * F_IN:4 * BATCH * F_IN + 2 * F_IN].rearrange("p (s f) -> p s f", f=F_IN)
        s_in = [counter(f"s_in{i}") for i in range(2)]
        y_out = [counter(f"y_out{i}") for i in range(2)]
        x1_out = [counter(f"x1_out{i}") for i in range(2)]
        table_dma = counter("table_dma")
        w2_ld = counter("ld_w2")
        w2_at = 0

        def rows_of(table, q):
            return table[q * BATCH * P:(q + 1) * BATCH * P, :].rearrange("(t p) f -> p t f", p=P)

        def c_load(q):
            if q < 2:
                D.wait(("agg", GROUPS - 4 + q, GROUP - 1))
            else:
                D.wait(("x1_out", q - 2))
            D.dma(lambda e: e.dma_start(s_all[:, q % 2, :, :], rows_of(x_plus_xn, q)), s_in[q % 2], ("s_in", q))

        def c_residual(q):
            t0 = q * BATCH
            hv = acc_t[:, t0:t0 + BATCH, 0:F_IN].rearrange("p t (h o) -> p t h o", o=F_OUT)
            if q == 0:
                V.wait("rsum")
            V.do(lambda e: e.tensor_tensor(
                hv, hv, rsum[:, t0:t0 + BATCH, :].unsqueeze(3).broadcast_to([P, BATCH, HEADS, F_OUT]),
                ALU.mult), ("C_gat", q))
            V.wait(("C_gat", q), ("s_in", q))
            V.do(lambda e: e.tensor_tensor(acc_t[:, t0:t0 + BATCH, 0:F_IN], acc_t[:, t0:t0 + BATCH, 0:F_IN],
                                           s_all[:, q % 2, :, :], ALU.add), ("C_x1", q))
            V.wait(("C_x1", q))
            many_stats("C", t0, lambda t: acc_t[:, t, 0:F_IN])
            var_std("C", t0, BATCH)

        def c_shift(q):
            t0 = q * BATCH
            inv_std("C", t0, BATCH)
            V.wait(("C", "rstd", t0))
            V.do(lambda e: e.scalar_tensor_tensor(shift[:, t0:t0 + BATCH], mean_var[:, t0:t0 + BATCH, 0], -1.0,
                                                  rstd[:, t0:t0 + BATCH], ALU.mult, ALU.mult), ("C_shift", q))

        def c_x1_beta(q):
            t0 = q * BATCH
            if q == 0:
                V.wait("b1")
            V.do(lambda e: e.tensor_tensor(s_all[:, q % 2, :, :], acc_t[:, t0:t0 + BATCH, 0:F_IN],
                                           beta_bc[:, :].unsqueeze(1).broadcast_to([P, BATCH, F_IN]), ALU.add),
                 ("C_x1b", q))
            D.wait(("C_x1b", q))
            D.dma(lambda e: e.dma_start(rows_of(x1_beta, q), s_all[:, q % 2, :, :]), x1_out[q % 2],
                  ("x1_out", q))

        def c_gate(t):
            q = t // BATCH
            S.wait(("C_ytr", t))
            if t >= 2:
                S.wait(("C_gate", t - 2))
            S.do(copy_s(yt_buf[:, t % 2, :], bank[4 + t % 2][:, 0:F_IN]), ("C_yt", t))
            T.wait(("C_yt", t))
            if q >= 2:
                T.wait(("C_logits", q - 2))
            lg = bank[2 + q % 2][:, (t % BATCH) * EXPERTS:(t % BATCH + 1) * EXPERTS]
            for c in range(KC):
                T.do(lambda e, t=t, c=c, lg=lg: e.matmul(lg, yt_buf[:, t % 2, c * P:(c + 1) * P],
                                                         gate_sb[:, c, :], start=(c == 0), stop=False))
            T.do(lambda e, lg=lg: e.matmul(lg, ones[0:1, :], gate_b_sb[:, :], start=False, stop=True),
                 ("C_gate", t))

        def c_norm(q):
            t0 = q * BATCH
            for t in range(t0, t0 + BATCH):
                S.wait(("C_shift", q))
                if q >= 2:
                    S.wait(("y_out", q - 2))
                S.do(lambda e, t=t: e.activation(y_all[:, q % 2, t % BATCH, :], acc_t[:, t, 0:F_IN],
                                                 ACT.Identity, bias=shift[:, t:t + 1], scale=rstd[:, t:t + 1]),
                     ("C_y0", t))
                T.wait(("C_y0", t))
                if t == 0:
                    T.wait("gate")
                if t >= 2:
                    T.wait(("C_yt", t - 2))
                for c in range(KC):
                    T.do(lambda e, t=t, c=c: e.transpose(
                        bank[4 + t % 2][:, c * P:(c + 1) * P],
                        y_all[:, q % 2, t % BATCH, c * P:(c + 1) * P], ident[:, :]),
                        ("C_ytr", t) if c == KC - 1 else None)
                if t > t0:
                    c_gate(t - 1)
            c_gate(t0 + BATCH - 1)
            D.wait(("C_y0", t0 + BATCH - 1))
            D.dma(lambda e: e.dma_start(rows_of(y0_rows, q), y_all[:, q % 2, :, :]), y_out[q % 2], ("y_out", q))

        def c_choose(q):
            t0 = q * BATCH
            V.wait(("C_gate", t0 + BATCH - 1))
            V.do(lambda e: e.tensor_copy(logits[:, t0:t0 + BATCH, :].rearrange("p t e -> p (t e)"),
                                         bank[2 + q % 2][:, 0:BATCH * EXPERTS]), ("C_logits", q))
            V.wait(("C_logits", q))
            for t in range(t0, t0 + BATCH):
                V.do(lambda e, t=t: e.max(top_v[:, t, :], logits[:, t, :]), ("C_top", t))
            for t in range(t0, t0 + BATCH):
                V.wait(("C_top", t))
                V.do(lambda e, t=t: e.max_index(top_i[:, t, :], top_v[:, t, :], logits[:, t, :]), ("C_idx", t))
            V.wait(("C_idx", t0 + BATCH - 1))
            V.do(lambda e: e.tensor_copy(top_f[:, :, :], top_i[:, t0:t0 + BATCH, 0:TOP_K]), ("C_topf", q))
            V.wait(("C_topf", q))
            if q >= 1:
                V.wait(("C_tot", q - 1), ("C_pos", q - 1))
            for k in range(TOP_K):
                V.do(lambda e, k=k: e.tensor_tensor(
                    chosen[:, k, :, :], iota_row[:, 0:EXPERTS].unsqueeze(1).broadcast_to([P, BATCH, EXPERTS]),
                    top_f[:, :, k:k + 1].broadcast_to([P, BATCH, EXPERTS]), ALU.is_equal), ("C_ch", q, k))
            V.wait(("C_ch", q, 1))
            V.do(lambda e: e.tensor_tensor(both[:, :, :], chosen[:, 0, :, :], chosen[:, 1, :, :], ALU.add),
                 ("C_both0", q))
            V.wait(("C_both0", q))
            if q == BATCHES - 1:
                V.do(lambda e: e.tensor_scalar(both[:, BATCH - 1, :], both[:, BATCH - 1, :], row_ok[:, :], None,
                                               ALU.mult), ("C_both", q))
            else:
                marks.put(("C_both", q), *marks.at[("C_both0", q)])
            T.wait(("C_both", q))
            if q >= 1:
                T.wait(("C_rank", q - 1), ("C_base", t0 - 1))
            flat = both[:, :, :].rearrange("p t e -> p (t e)")
            T.do(lambda e: e.matmul(bank[7][:, 0:BATCH * EXPERTS], ones[:, :], flat, start=True, stop=True),
                 ("C_tot", q))
            T.do(lambda e: e.matmul(bank[6][:, 0:BATCH * EXPERTS], before[:, :], flat, start=True, stop=True),
                 ("C_bef", q))

        def c_slots(q):
            t0 = q * BATCH
            V.wait(("C_tot", q), "base0")
            for t in range(t0, t0 + BATCH):
                if t > 0:
                    V.wait(("C_base", t - 1))
                o = (t - t0) * EXPERTS
                V.do(lambda e, t=t, o=o: e.tensor_tensor(base[:, t + 1, :], base[:, t, :],
                                                         bank[7][:, o:o + EXPERTS], ALU.add), ("C_base", t))
            V.wait(("C_base", t0 + BATCH - 1), ("C_bef", q))
            V.do(lambda e: e.tensor_tensor(rank[:, :, :], base[:, t0:t0 + BATCH, :],
                                           bank[6][:, 0:BATCH * EXPERTS].rearrange("p (t e) -> p t e",
                                                                                   e=EXPERTS), ALU.add),
                 ("C_rank", q))
            V.wait(("C_rank", q))
            V.do(lambda e: e.tensor_tensor(picked[:, :, :, :], chosen[:, :, :, :],
                                           rank[:, :, :].unsqueeze(1).broadcast_to([P, TOP_K, BATCH, EXPERTS]),
                                           ALU.mult), ("C_pick", q))
            V.wait(("C_pick", q))
            V.do(lambda e: e.tensor_reduce(pos_f[:, :, :], picked[:, :, :, :], AXIS_FREE, ALU.add),
                 ("C_posf", q))
            V.wait(("C_posf", q))
            V.do(lambda e: e.tensor_copy(pos_i[:, :, t0:t0 + BATCH], pos_f[:, :, :]), ("C_pos", q))

        def c_scatter(q):
            G.wait(("C_pos", q), "table0", "dest")
            for t in range(q * BATCH, (q + 1) * BATCH):
                rows = P if t < TILES - 1 else LAST_ROWS
                for k in range(TOP_K):
                    G.dma(lambda e, t=t, k=k, rows=rows: e.indirect_dma_start(
                        slot_table, bass.IndirectOffsetOnAxis(pos_i[0:rows, k, t:t + 1], 0),
                        dest_i[0:rows, t, k:k + 1], None), table_dma,
                        ("table", t) if k == TOP_K - 1 else None)

        def c_w2(q):
            nonlocal w2_at
            done = BATCH * (q + 1)
            while w2_at < EXPERTS and ((w2_at + 1) * FC * F_IN <= done * ROW or done == TILES):
                x_ = w2_at
                D.dma(lambda e, x_=x_: e.dma_start(
                    w2_sb.rearrange("p (x c f) -> p x c f", c=FC, f=F_IN)[:, x_, :, :],
                    w2[x_, :, :].rearrange("(c p) f -> p c f", p=P)), w2_ld,
                    "w2" if x_ == EXPERTS - 1 else None)
                w2_at += 1

        c_load(0)
        c_load(1)
        c_residual(0)
        c_x1_beta(0)
        c_shift(0)
        c_norm(0)
        for q in range(BATCHES):
            if q + 1 < BATCHES:
                c_residual(q + 1)
            c_choose(q)
            if q + 1 < BATCHES:
                c_x1_beta(q + 1)
                c_shift(q + 1)
            c_slots(q)
            c_scatter(q)
            if q + 1 < BATCHES:
                c_norm(q + 1)
            c_w2(q)
            if q + 2 < BATCHES:
                c_load(q + 2)
        b2_ld = counter("ld_b2")
        D.wait("gap", "d0")
        D.dma(lambda e: e.dma_start(b2_bc, b2.rearrange("x f -> (x f)").partition_broadcast(P)), b2_ld, "b2")

        V.wait(("C_top", TILES - 1))
        V.do(lambda e: e.tensor_tensor(gap[:, :], top_v[:, :, 1], top_v[:, :, 0], ALU.subtract), "gap")
        S.wait("gap")
        S.do(lambda e: e.activation(weight[:, 1, :], gap[:, :], ACT.Exp), "gap_exp")
        V.wait("gap_exp")
        V.do(lambda e: e.tensor_scalar(gap[:, :], weight[:, 1, :], 1.0, None, ALU.add), "gap1")
        V.wait("gap1")
        V.do(lambda e: e.reciprocal(weight[:, 0, :], gap[:, :]), "weight0")
        V.wait("weight0")
        V.do(lambda e: e.tensor_tensor(weight[:, 1, :], weight[:, 1, :], weight[:, 0, :], ALU.mult), "weight1")

        V.wait(("C_base", TILES - 1))
        V.do(lambda e: e.tensor_tensor(cnt_f[:, :], base[:, TILES, :], base[:, 0, :], ALU.subtract), "d0")
        V.wait("d0")
        V.do(lambda e: e.tensor_scalar(cnt_f[:, :], cnt_f[:, :], float(P - 1), None, ALU.add), "d1")
        V.wait("d1")
        V.do(lambda e: e.tensor_copy(cnt_i[:, :], cnt_f[:, :]), "d2")
        V.wait("d2")
        V.do(lambda e: e.tensor_scalar(cnt_i[:, :], cnt_i[:, :], 7, None, ALU.arith_shift_right), "d3")
        V.wait("d3")
        V.do(lambda e: e.tensor_copy(ntile[:, :], cnt_i[:, :]), "d4")
        V.wait("d4")
        V.do(lambda e: e.tensor_tensor_scan(incl[:, :], ones[:, 0:EXPERTS], ntile[:, :], 0.0, ALU.mult,
                                            ALU.add), "d5")
        V.wait("d5")
        V.do(lambda e: e.tensor_tensor(excl[:, :], incl[:, :], ntile[:, :], ALU.subtract), "d6")
        V.do(lambda e: e.tensor_scalar(smalls[:, :], incl[:, :], iota_col[:, :], 0.0, ALU.is_le, ALU.add,
                                       accum_out=small[:, 0:1]), "d7")
        V.wait("d7", "d6")
        V.do(lambda e: e.scalar_tensor_tensor(smalls[:, :], iota_row[:, 0:EXPERTS], small[:, 0:1], excl[:, :],
                                              ALU.is_equal, ALU.mult, accum_out=small[:, 1:2]), "d8")
        V.wait("d8")
        V.do(lambda e: e.tensor_tensor(small[:, 2:3], iota_col[:, :], small[:, 1:2], ALU.subtract), "d9")
        V.wait("d9")
        V.do(lambda e: e.scalar_tensor_tensor(small[:, 3:4], small[:, 0:1], float(TILES), small[:, 2:3],
                                              ALU.mult, ALU.add), "d10")
        V.wait("d10")
        V.do(lambda e: e.tensor_scalar(small[:, 4:5], small[:, 3:4], float(BLOCKS), None, ALU.min), "d11")
        V.do(lambda e: e.tensor_scalar(small[:, 5:6], small[:, 0:1], float(EXPERTS - 1), None, ALU.min), "d12")
        V.wait("d11")
        V.do(lambda e: e.tensor_copy(blk_i[:, :], small[:, 4:5]), "blk")
        slots_d = counter("slots_dma")
        G.wait("blk", ("table", TILES - 1))
        G.dma(lambda e: e.indirect_dma_start(slots_i[:, :], None, slot_table.rearrange("(b s) o -> b (s o)", s=P),
                                             bass.IndirectOffsetOnAxis(blk_i[:, :], 0)), slots_d, "slots")
        T.wait("d12", "eps")
        T.do(lambda e: e.transpose(bank[0][0:1, 0:P], small[:, 5:6], ident[:, :]), "ex_tr")
        V.wait("ex_tr")
        V.do(lambda e: e.tensor_copy(expert_row[:, :], bank[0][0:1, 0:P]), "expert_row")
        V.wait("slots")
        V.do(lambda e: e.tensor_copy(slots_f[:, :], slots_i[:, :]), "slots_f")
        T.wait("slots_f")
        T.do(lambda e: e.transpose(bank[1][:, 0:P], slots_f[:, :], ident[:, :]), "slots_tr")
        V.wait("slots_tr")
        V.do(lambda e: e.tensor_copy(dest_u[:, :], bank[1][:, 0:P]), "dest_u")
        V.wait("dest_u")
        V.do(lambda e: e.tensor_scalar(token_u[:, :], dest_u[:, :], 1, None, ALU.logical_shift_right), "tok0")
        V.wait("tok0")
        V.do(lambda e: e.tensor_scalar(token_u[:, :], token_u[:, :], float(NODES - 1), None, ALU.min), "token")

        XG = 4
        at = 0

        def take(n, w):
            nonlocal at
            v = region2[:, at:at + n * w].rearrange("p (s f) -> p s f", f=w)
            at += n * w
            return v
        xg_buf, xgt_buf = take(XG, F_IN), take(2, F_IN)
        w1_buf, hidt_buf, y_buf = take(2, KC * HIDDEN), take(2, HIDDEN), take(3, F_IN)
        xg_in = [counter(f"xg_in{i}") for i in range(XG)]
        yb_out = [counter(f"yb_out{i}") for i in range(3)]
        flat_w1 = w1_sb
        flat_w2 = w2_sb

        def d_gather(j):
            if j == 0:
                G.wait("token")
                for q in (BATCHES - 2, BATCHES - 1):
                    G.wait(("y_out", q), ("x1_out", q))
            if j >= XG:
                G.wait(("D_xtr", j - XG))
            G.dma(lambda e: e.indirect_dma_start(xg_buf[:, j % XG, :], None, y0_rows,
                                                 bass.IndirectOffsetOnAxis(token_u[:, j:j + 1], 0)),
                  xg_in[j % XG], ("xg", j))

        def d_scatter(j):
            G.wait(("D_y", j))
            G.dma(lambda e: e.indirect_dma_start(
                choice_rows, bass.IndirectOffsetOnAxis(dest_u[:, j:j + 1], 0), y_buf[:, j % 3, :], None,
                bounds_check=NODES * TOP_K - 1, oob_is_err=False), yb_out[j % 3], ("yb_out", j))

        X_BANKS, HIDT_BANKS, Y_BANKS = (0, 1), (2, 3), (6, 7)

        def d_xtr(j):
            T.wait(("xg", j))
            if j == 0:
                T.wait("dest_u", "expert_row")
            if j >= 2:
                T.wait(("D_xt", j - 2))
            for c in range(KC):
                T.do(lambda e, c=c: e.transpose(bank[X_BANKS[j % 2]][:, c * P:(c + 1) * P],
                                                xg_buf[:, j % XG, c * P:(c + 1) * P], ident[:, :]),
                     ("D_xtr", j) if c == KC - 1 else None)
            V.wait(("D_xtr", j))
            if j >= 2:
                V.wait(("D_l1", j - 2))
            V.do(lambda e: e.tensor_copy(xgt_buf[:, j % 2, :], bank[X_BANKS[j % 2]][:, 0:F_IN]), ("D_xt", j))

        experts = {}

        def load_experts(queue, use, j):
            if j % GROUP == 0:
                n = min(GROUP, SLOT_TILES - j)

                def load(e):
                    _, experts[use] = nc.values_load_multi_w_load_instructions(
                        expert_row[0:1, j:j + n], engines=[e.engine], min_val=0, max_val=EXPERTS - 1,
                        skip_runtime_bounds_check_because="the value was clamped on chip")
                if j == 0:
                    queue.wait("expert_row")
                queue.do(load)

        def d_weights(j):
            if j == 0:
                V.wait("w1")
            if j >= 2:
                V.wait(("D_l1", j - 2))
            load_experts(V, "weights", j)

            def emit(e):
                x_ = experts["weights"][j % GROUP]
                return e.tensor_copy(w1_buf[:, j % 2, :],
                                     flat_w1[:, bass.ds(x_ * (KC * HIDDEN), KC * HIDDEN)])
            V.do(emit, ("D_w1", j))

        def d_layer1(j):
            T.wait(("D_xt", j), ("D_w1", j))
            if j >= 2:
                T.wait(("D_ht", j - 2))
            for f in range(FC):
                for c in range(KC):
                    T.do(lambda e, f=f, c=c: e.matmul(
                        bank[HIDT_BANKS[j % 2]][:, f * P:(f + 1) * P],
                        w1_buf[:, j % 2, c * HIDDEN + f * P:c * HIDDEN + (f + 1) * P],
                        xgt_buf[:, j % 2, c * P:(c + 1) * P], start=(c == 0), stop=(c == KC - 1)),
                        ("D_l1", j) if f == FC - 1 and c == KC - 1 else None)
            S.wait(("D_l1", j))
            if j == 0:
                S.wait("b1_col")
            if j >= 2:
                S.wait(("D_l2", j - 2))

            load_experts(S, "b1", j)

            def emit_s(e):
                x_ = experts["b1"][j % GROUP]
                flat_b1 = b1_col[:, :, :].rearrange("p c e -> p (c e)")
                for f in range(FC):
                    ins = e.activation(hidt_buf[:, j % 2, f * P:(f + 1) * P],
                                       bank[HIDT_BANKS[j % 2]][:, f * P:(f + 1) * P], ACT.Relu,
                                       bias=flat_b1[:, bass.ds(x_ + f * EXPERTS, 1)])
                return ins
            S.do(emit_s, ("D_ht", j))

        def d_layer2(j):
            T.wait(("D_ht", j))
            if j == 0:
                T.wait("w2")
            if j >= 2:
                T.wait(("D_y", j - 2))

            load_experts(T, "w2", j)

            def emit(e):
                x_ = experts["w2"][j % GROUP]
                for f in range(FC):
                    ins = e.matmul(bank[Y_BANKS[j % 2]][:, 0:F_IN], hidt_buf[:, j % 2, f * P:(f + 1) * P],
                                   flat_w2[:, bass.ds(x_ * (FC * F_IN) + f * F_IN, F_IN)],
                                   start=(f == 0), stop=(f == FC - 1))
                return ins
            T.do(emit, ("D_l2", j))
            V.wait(("D_l2", j))
            if j == 0:
                V.wait("b2")
            if j >= 3:
                V.wait(("yb_out", j - 3))

            load_experts(V, "b2", j)

            def emit_y(e):
                x_ = experts["b2"][j % GROUP]
                return e.tensor_tensor(y_buf[:, j % 3, :], bank[Y_BANKS[j % 2]][:, 0:F_IN],
                                       b2_bc[:, bass.ds(x_ * F_IN, F_IN)], ALU.add)
            V.do(emit_y, ("D_y", j))

        for j in range(XG - 1):
            d_gather(j)
        for j in range(2):
            d_xtr(j)
            d_weights(j)
        for i in range(SLOT_TILES + 1):
            if i < SLOT_TILES:
                d_layer1(i)
            if i + 2 < SLOT_TILES:
                d_xtr(i + 2)
                d_weights(i + 2)
            if i >= 1:
                d_layer2(i - 1)
            if i + XG - 1 < SLOT_TILES:
                d_gather(i + XG - 1)
            if i >= 1:
                d_scatter(i - 1)

        n_e = BATCH * F_IN
        e_slot = [region0[:, s * 4 * n_e:(s + 1) * 4 * n_e] for s in range(2)]
        e_y0 = [v[:, 0:n_e].rearrange("p (t f) -> p t f", f=F_IN) for v in e_slot]
        e_x1 = [v[:, n_e:2 * n_e].rearrange("p (t f) -> p t f", f=F_IN) for v in e_slot]
        e_ch = [v[:, 2 * n_e:4 * n_e].rearrange("p (t k f) -> p t k f", k=TOP_K, f=F_IN) for v in e_slot]
        e_in = [counter(f"e_in{i}") for i in range(2)]
        e_chin = [counter(f"e_chin{i}") for i in range(2)]
        out_d = [counter(f"out{i}") for i in range(2)]
        for q in range(BATCHES):
            s = q % 2
            full = BATCH if q < BATCHES - 1 else BATCH - 1
            t0 = q * BATCH
            if q == 0:
                D.wait(("D_l1", SLOT_TILES - 1))
            if q >= 2:
                D.wait(("out", q - 2), ("E_g", t0 - BATCH - 1))
            D.dma(lambda e, q=q, s=s: e.dma_start(e_y0[s], rows_of(y0_rows, q)), e_in[s], None)
            D.dma(lambda e, q=q, s=s: e.dma_start(e_x1[s], rows_of(x1_beta, q)), e_in[s], ("e_in", q))
            if q == 0:
                for j in range(SLOT_TILES - 3, SLOT_TILES):
                    D.wait(("yb_out", j))
            D.dma(lambda e, q=q, s=s, full=full, t0=t0: e.dma_start(
                e_ch[s][:, 0:full, :, :].rearrange("p t k f -> p t (k f)"),
                choice_rows[t0 * P * TOP_K:(t0 + full) * P * TOP_K, :].rearrange(
                    "(t p k) f -> p t (k f)", p=P, k=TOP_K)), e_chin[s],
                ("e_ch", q) if full == BATCH else None)
            if full < BATCH:
                V.wait(("E_y", t0 - BATCH - 1))
                V.do(lambda e, s=s: e.memset(e_ch[s][:, BATCH - 1, :, :], 0.0), "e_tail")
                D.wait("e_tail")
                D.dma(lambda e, s=s: e.dma_start(
                    e_ch[s][0:LAST_ROWS, BATCH - 1, :, :].rearrange("p k f -> p (k f)"),
                    choice_rows[(TILES - 1) * P * TOP_K:NODES * TOP_K, :].rearrange(
                        "(p k) f -> p (k f)", k=TOP_K)), e_chin[s], ("e_ch", q))
            V.wait(("e_in", q), ("e_ch", q), "weight1")
            for t in range(t0, t0 + BATCH):
                k = t % BATCH
                y = e_y0[s][:, k, :]
                V.do(lambda e, s=s, k=k, t=t, y=y: e.scalar_tensor_tensor(
                    y, e_ch[s][:, k, 0, :], weight[:, 0, t:t + 1], y, ALU.mult, ALU.add), ("E_1", t))
                V.wait(("E_1", t))
                V.do(lambda e, s=s, k=k, t=t, y=y: e.scalar_tensor_tensor(
                    y, e_ch[s][:, k, 1, :], weight[:, 1, t:t + 1], y, ALU.mult, ALU.add), ("E_y", t))
                V.wait(("E_y", t))
                stats_of("E", t, y)
            rstd_of("E", t0, BATCH)
            V.wait(("E", "rstd", t0))
            V.do(lambda e, t0=t0: e.scalar_tensor_tensor(
                shift[:, t0:t0 + BATCH], mean_var[:, t0:t0 + BATCH, 0], -1.0, rstd[:, t0:t0 + BATCH],
                ALU.mult, ALU.mult), ("E_shift", q))
            for t in range(t0, t0 + BATCH):
                k = t % BATCH
                S.wait(("E_shift", q))
                S.do(lambda e, s=s, k=k, t=t: e.activation(
                    e_y0[s][:, k, :], e_y0[s][:, k, :], ACT.Identity, bias=shift[:, t:t + 1],
                    scale=rstd[:, t:t + 1]), ("E_n", t))
                G.wait(("E_n", t))
                G.do(lambda e, s=s, k=k: e.tensor_tensor(e_y0[s][:, k, :], e_y0[s][:, k, :], gamma_bc[:, :],
                                                         ALU.mult), ("E_g0", t))
                G.wait(("E_g0", t))
                G.do(lambda e, s=s, k=k: e.tensor_tensor(e_y0[s][:, k, :], e_y0[s][:, k, :], e_x1[s][:, k, :],
                                                         ALU.add), ("E_g", t))
            S.wait(("E_g", t0 + BATCH - 1))
            S.dma(lambda e, q=q, s=s, full=full, t0=t0: e.dma_start(
                out[t0 * P:(t0 + full) * P, :].rearrange("(t p) f -> p t f", p=P), e_y0[s][:, 0:full, :]),
                out_d[s], ("out", q) if full == BATCH else None)
            if full < BATCH:
                S.dma(lambda e, s=s: e.dma_start(out[(TILES - 1) * P:NODES, :],
                                                 e_y0[s][0:LAST_ROWS, BATCH - 1, :]), out_d[s], ("out", q))
        S.wait(("out", BATCHES - 2), ("out", BATCHES - 1))

        block = ctx.enter_context(nc.Block())

        @block.sync
        def _(eng):
            D.emit(eng)

        @block.scalar
        def _(eng):
            S.emit(eng)

        @block.gpsimd
        def _(eng):
            G.emit(eng)

        @block.tensor
        def _(eng):
            T.emit(eng)

        @block.vector
        def _(eng):
            V.emit(eng)


_INS = ["x", "src", "dst", "L0_gnn_W", "L0_gnn_a_src", "L0_gnn_a_dst", "L0_ffn_gate_w", "L0_ffn_gate_b",
        "L0_ffn_w1", "L0_ffn_b1", "L0_ffn_w2", "L0_ffn_b2", "L0_ffn_gamma", "L0_ffn_beta"]


def kernel(**inputs):
    import numpy as _np
    import concourse.bacc as _bacc
    from concourse import mybir as _mybir
    from concourse.bass_utils import run_bass_kernel_spmd as _run

    nc = _bacc.Bacc("TRN2", target_bir_lowering=False, num_devices=1)
    arrays, args = {}, []
    for name in _INS:
        a = _np.ascontiguousarray(inputs[name])
        arrays[f"in_{name}"] = a
        args.append(nc.dram_tensor(f"in_{name}", a.shape, _mybir.dt.from_np(a.dtype), kind="ExternalInput").ap())
    args.append(nc.dram_tensor("out", (NODES, F_IN), _mybir.dt.float32, kind="ExternalOutput").ap())
    build_program(nc, *args)
    r = _run(nc, [arrays], core_ids=[0])
    return r.results[0]["out"]
```

```python
from contextlib import ExitStack

import concourse.bass as bass
from concourse import mybir
from concourse.alu_op_type import AluOpType as ALU

ACT = mybir.ActivationFunctionType
AXIS_FREE = mybir.AxisListType.X
F32 = mybir.dt.float32
I32 = mybir.dt.int32
U32 = mybir.dt.uint32

P = 128
NODES = 6250
EDGES = 100000
HEADS, F_IN, F_OUT = 8, 256, 32
EXPERTS, HIDDEN, TOP_K = 16, 512, 2
LN_EPS = 1e-5
SUM_EPS = 1e-10
SLOPE = 0.2
FAR_BELOW = -1e30
EXP_TOP = 80.0

TILES = -(-NODES // P)
LAST_ROWS = NODES - (TILES - 1) * P
CHUNKS = -(-EDGES // P)
GROUP = 8
GROUPS = -(-(CHUNKS + TILES - 1) // GROUP)
STEPS = GROUPS * GROUP
STEP_BLOCKS = -(-STEPS // P)
ROW = F_IN + HEADS
AD = HEADS + 1
BATCH = 7
BATCHES = TILES // BATCH
SLOT_TILES = (NODES * TOP_K + EXPERTS * (P - 1)) // P
BLOCKS = EXPERTS * TILES
NO_ROW = 1 << 20
KC = F_IN // P
FC = HIDDEN // P

assert TILES % BATCH == 0 and SLOT_TILES <= P and ROW <= 512


class Marks:

    def __init__(self):
        self.at = {}

    def put(self, name, sem, value):
        assert name not in self.at, name
        self.at[name] = (sem, value)


class Queue:

    def __init__(self, marks, sem):
        self.marks, self.sem, self.count, self.items = marks, sem, 0, []

    def do(self, emit, name=None):
        if name is not None:
            self.count += 1
            self.marks.put(name, self.sem, self.count)
        self.items.append(("do", emit, self.sem if name is not None else None))

    def dma(self, emit, counter, name):
        counter[1] += 16
        if name is not None:
            self.marks.put(name, counter[0], counter[1])
        self.items.append(("dma", emit, counter[0]))

    def wait(self, *names):
        for name in names:
            self.items.append(("wait", name, None))

    def emit(self, eng):
        passed = {}
        for kind, what, sem in self.items:
            if kind == "wait":
                s, value = self.marks.at[what]
                if passed.get(s.name, 0) < value:
                    eng.wait_ge(s, value)
                    passed[s.name] = value
            else:
                ins = what(eng)
                if sem is not None:
                    ins.then_inc(sem, 16 if kind == "dma" else 1)


def build_program(nc, x, src, dst, w_gnn, a_src, a_dst, gate_w, gate_b, w1, b1, w2, b2, gamma, beta, out):
    ctx = ExitStack()
    with ctx:
        ctx.enter_context(nc.allow_non_contiguous_dma(reason="one dst per chunk, few and small"))

        def sb(name, shape, dt=F32):
            return ctx.enter_context(nc.sbuf_tensor(name, shape, dt))

        def dram(name, shape, dt=F32):
            return nc.dram_tensor(name, shape, dt, kind="Internal").ap()

        def sem(name):
            return ctx.enter_context(nc.semaphore(name))

        def counter(name):
            return [sem(name), 0]

        node_rows = dram("node_rows", [TILES * P, ROW])
        x_plus_xn = dram("x_plus_xn", [TILES * P, F_IN])
        x1_rows = dram("x1_rows", [TILES * P, F_IN])
        y0_rows = dram("y0_rows", [TILES * P, F_IN])
        choice_rows = dram("choice_rows", [TILES * P * TOP_K, F_IN])
        src_pad = dram("src_pad", [CHUNKS * P], I32)
        dst_pad = dram("dst_pad", [CHUNKS * P], I32)
        slot_table = dram("slot_table", [(BLOCKS + 1) * P, 1], I32)

        region0 = sb("region0", [P, EXPERTS * KC * HIDDEN])
        region1 = sb("region1", [P, EXPERTS * FC * F_IN])
        region2 = sb("region2", [P, 7 * 1024 + 512])
        region3 = sb("region3", [P, 2 * STEPS + 24 * P])
        x_all = region0[:, 0:TILES * F_IN].rearrange("p (t f) -> p t f", f=F_IN)
        w1_sb = region0[:, :]
        w2_sb = region1[:, :]
        acc = region1[:, 0:TILES * ROW]
        acc_t = acc.rearrange("p (t c) -> p t c", c=ROW)
        over_chunks = region1[:, 0:10 * CHUNKS].rearrange("p (n c) -> p n c", c=CHUNKS)
        first_bc, delta_bc, iota_chunk, junk = [over_chunks[:, n, :] for n in range(4)]
        row_a, row_b, row_c, row_d = [over_chunks[0:1, n, :] for n in range(4, 8)]
        ends_i = over_chunks[0:1, 8:10, :].bitcast(I32)
        blank = region1[0:BLOCKS // BATCH, 10 * CHUNKS:10 * CHUNKS + BATCH * P].bitcast(I32)
        behind = TILES * ROW

        def next_behind(parts, width):
            nonlocal behind
            behind += width
            return region1[0:parts, behind - width:behind]
        rows_at = 3072 + 8 * ROW
        rows_i = region2[:, rows_at:rows_at + 2 * STEP_BLOCKS * P].rearrange("p (s m) -> p s m", m=P).bitcast(I32)
        rows_f = next_behind(P, 4 * P).rearrange("p (s m) -> p s m", m=P)
        w_cat = next_behind(P, KC * (ROW + HEADS)).rearrange("p (c m) -> p c m", c=KC)
        a_bc = next_behind(P, 2 * F_IN).rearrange("p (n f) -> p n f", n=2)
        b1_rows = next_behind(EXPERTS, HIDDEN)
        pad_i = next_behind(1, 2 * P).bitcast(I32)
        assert behind <= EXPERTS * FC * F_IN
        dloc = region3[:, 0:STEPS]
        src_idx = region3[:, STEPS:2 * STEPS].bitcast(U32)
        oh_base = 2 * STEPS
        onehot = region3[:, oh_base:oh_base + 24 * P].rearrange("p (s m) -> p s m", m=P)
        onehot_t = region1[:, TILES * ROW:TILES * ROW + 8 * P].rearrange("p (s m) -> p s m", m=P)
        b2_bc = region3[:, 0:EXPERTS * F_IN]
        cut = [0, TILES * EXPERTS, TILES * 8, TILES * 8, (TILES + 1) * EXPERTS]
        logits, top_v, top_i, base = [
            region3[:, sum(cut[:n + 1]):sum(cut[:n + 2])].rearrange("p (t e) -> p t e", e=e)
            for n, e in enumerate((EXPERTS, 8, 8, EXPERTS))]
        top_i = top_i.bitcast(U32)

        iota_row_i = sb("iota_row_i", [P, P], I32)
        iota_row = sb("iota_row", [P, P])
        iota_col_i = sb("iota_col_i", [P, 1], I32)
        iota_col = sb("iota_col", [P, 1])
        ident = sb("ident", [P, P])
        before = sb("before", [P, P])
        ones = sb("ones", [P, P])
        kcol_i = sb("kcol_i", [P, STEP_BLOCKS], I32)
        kcol = sb("kcol", [P, STEP_BLOCKS])
        step_c = sb("step_c", [P, STEP_BLOCKS])
        step_ci = sb("step_ci", [P, STEP_BLOCKS], U32)
        step_d = sb("step_d", [P, STEP_BLOCKS])
        step_t = sb("step_t", [P, STEP_BLOCKS])
        step_t128 = sb("step_t128", [P, STEP_BLOCKS])
        step_tc = sb("step_tc", [P, STEP_BLOCKS])
        tile_row = sb("tile_row", [1, STEP_BLOCKS * P], I32)
        tfirst = sb("tfirst", [1, GROUPS])
        tile_base = sb("tile_base", [P, TILES, AD])
        stats = sb("stats", [P, BATCH, 6])
        mean_var = sb("mean_var", [P, TILES, 2])
        var_eps = sb("var_eps", [P, TILES])
        std = sb("std", [P, TILES])
        rstd = sb("rstd", [P, TILES])
        shift = sb("shift", [P, TILES])
        neg_max = sb("neg_max", [P, GROUPS + 1])
        run_max = sb("run_max", [1, GROUPS + 1])
        fall = sb("fall", [P, GROUPS])
        z = sb("z", [P, 2, GROUP, HEADS])
        cap = sb("cap", [P, 2, GROUP])
        zmax = sb("zmax", [P, 2])
        gmax = sb("gmax", [1, 2])
        late = sb("late", [P, GROUPS])
        late_min = sb("late_min", [P, 1])
        eps_row = sb("eps_row", [1, P])
        eps_bc = sb("eps_bc", [P, TILES])
        rsum = sb("rsum", [P, TILES, HEADS])
        rstd_y = sb("rstd_y", [P, TILES])
        shift_y = sb("shift_y", [P, TILES])
        gate_sb = sb("gate_sb", [P, KC, EXPERTS])
        gate_b_bc = sb("gate_b_bc", [P, EXPERTS])
        top_f = sb("top_f", [P, BATCH, TOP_K])
        chosen = sb("chosen", [P, TOP_K, BATCH, EXPERTS])
        both = sb("both", [P, BATCH, EXPERTS])
        rank = sb("rank", [P, BATCH, EXPERTS])
        picked = sb("picked", [P, TOP_K, BATCH, EXPERTS])
        pos_f = sb("pos_f", [P, TOP_K, BATCH])
        pos_i = sb("pos_i", [P, TOP_K, TILES], U32)
        dest_i = sb("dest_i", [P, TILES, TOP_K], I32)
        row_ok = sb("row_ok", [P, 1])
        weight = sb("weight", [P, TOP_K, TILES])
        gap = sb("gap", [P, TILES])
        cnt_f = sb("cnt_f", [P, EXPERTS])
        cnt_i = sb("cnt_i", [P, EXPERTS], I32)
        ntile = sb("ntile", [P, EXPERTS])
        incl = sb("incl", [P, EXPERTS])
        excl = sb("excl", [P, EXPERTS])
        small = sb("small", [P, 6])
        smalls = sb("smalls", [P, EXPERTS])
        blk_i = sb("blk_i", [P, 1], U32)
        expert_row = sb("expert_row", [1, P], I32)
        slots_i = sb("slots_i", [P, P], I32)
        slots_f = sb("slots_f", [P, P])
        dest_u = sb("dest_u", [P, P], U32)
        token_u = sb("token_u", [P, P], U32)
        b1_col = sb("b1_col", [P, FC, EXPERTS])
        gamma_bc = sb("gamma_bc", [P, F_IN])
        beta_bc = sb("beta_bc", [P, F_IN])

        bank = [ctx.enter_context(nc.psum_tensor(f"bank{i}", [P, 512], F32)) for i in range(8)]

        marks = Marks()
        V = Queue(marks, sem("vector_done"))
        S = Queue(marks, sem("scalar_done"))
        T = Queue(marks, sem("tensor_done"))
        G = Queue(marks, sem("pool_done"))
        D = Queue(marks, sem("sync_done"))

        def copy_s(out_, in_):
            return lambda e: e.activation(out_, in_, ACT.Copy)

        ld = {n: counter(f"ld_{n}") for n in ("dstcopy", "srccopy", "ends", "wg", "gate", "b1")}
        D.dma(lambda e: e.dma_start(dst_pad[0:EDGES].rearrange("(a b) -> a b", a=16),
                                    dst.rearrange("(a b) -> a b", a=16)), ld["dstcopy"], None)
        D.dma(lambda e: e.dma_start(src_pad[0:EDGES].rearrange("(a b) -> a b", a=16),
                                    src.rearrange("(a b) -> a b", a=16)), ld["srccopy"], None)
        D.dma(lambda e: e.dma_start(ends_i[:, 0, :], dst.rearrange("(a n) -> a n", a=1)[:, 0:EDGES:P]),
              ld["ends"], None)
        D.dma(lambda e: e.dma_start(ends_i[:, 1, 0:CHUNKS - 1],
                                    dst.rearrange("(a n) -> a n", a=1)[:, P - 1:EDGES:P]), ld["ends"], None)
        D.dma(lambda e: e.dma_start(ends_i[:, 1, CHUNKS - 1:CHUNKS],
                                    dst.rearrange("(a n) -> a n", a=1)[:, EDGES - 1:EDGES]), ld["ends"], "ends")
        for c in range(KC):
            D.dma(lambda e, c=c: e.dma_start(w_cat[:, c, 0:F_IN].rearrange("p (h o) -> p h o", o=F_OUT),
                                             w_gnn[:, c * P:(c + 1) * P, :].rearrange("h p o -> p h o")),
                  ld["wg"], None)
        for n, a in enumerate((a_src, a_dst)):
            D.dma(lambda e, n=n, a=a: e.dma_start(
                a_bc[:, n, :], a.rearrange("h o x -> (x h o)").partition_broadcast(P)), ld["wg"], "wg" if n == 1 else None)
        xl = [counter(f"ld_x{q}") for q in range(BATCHES)]
        V.do(lambda e: e.memset(x_all[:, TILES - 1, :], 0.0), "x_tail")
        for q in range(BATCHES):
            full = BATCH if q < BATCHES - 1 else BATCH - 1
            r0 = q * BATCH * P
            D.dma(lambda e, q=q, full=full, r0=r0: e.dma_start(
                x_all[:, q * BATCH:q * BATCH + full, :],
                x[r0:r0 + full * P, :].rearrange("(t p) f -> p t f", p=P)), xl[q],
                ("x", q) if full == BATCH else None)
        D.wait("x_tail")
        D.dma(lambda e: e.dma_start(x_all[0:LAST_ROWS, TILES - 1, :], x[(TILES - 1) * P:NODES, :]),
              xl[BATCHES - 1], ("x", BATCHES - 1))

        G.do(lambda e: e.memset(pad_i[:, 0:P], 0), None)
        G.do(lambda e: e.memset(pad_i[:, P:2 * P], -1), "pad")
        G.do(lambda e: e.iota(iota_row_i[:, :], [[1, P]], base=0, channel_multiplier=0))
        G.do(lambda e: e.iota(iota_col_i[:, :], [[0, 1]], base=0, channel_multiplier=1))
        G.do(lambda e: e.iota(kcol_i[:, :], [[P, STEP_BLOCKS]], base=0, channel_multiplier=1))
        G.do(lambda e: e.iota(junk.bitcast(I32), [[1, CHUNKS]], base=0, channel_multiplier=0), "iotas")
        G.do(lambda e: e.memset(blank[:, :], NO_ROW), "blank")
        G.do(lambda e: e.iota(dest_i[:, :, :], [[2 * P, TILES], [1, TOP_K]], base=0, channel_multiplier=2),
             "dest")

        S.wait("pad")
        tail = CHUNKS * P - EDGES
        S.dma(lambda e: e.dma_start(src_pad[EDGES:].rearrange("(a n) -> a n", a=1), pad_i[:, 0:tail]),
              ld["srccopy"], "src_pad")
        S.dma(lambda e: e.dma_start(dst_pad[EDGES:].rearrange("(a n) -> a n", a=1), pad_i[:, P:P + tail]),
              ld["dstcopy"], "dst_pad")
        S.dma(lambda e: e.dma_start(gate_sb[:, :, :], gate_w.rearrange("(c p) e -> p c e", p=P)),
              ld["gate"], None)
        S.dma(lambda e: e.dma_start(gate_b_bc[:, :], gate_b.partition_broadcast(P)), ld["gate"], "gate")
        S.dma(lambda e: e.dma_start(b1_rows[:, :], b1), ld["b1"], None)
        S.dma(lambda e: e.dma_start(gamma_bc[:, :], gamma.partition_broadcast(P)), ld["b1"], None)
        S.dma(lambda e: e.dma_start(beta_bc[:, :], beta.partition_broadcast(P)), ld["b1"], "b1")
        tb = counter("blank_dma")
        S.wait("blank")
        S.dma(lambda e: e.dma_start(
            slot_table[0:BLOCKS * P, :].rearrange("(p n) o -> p (n o)", n=BATCH * P), blank[:, :]), tb, None)
        S.dma(lambda e: e.dma_start(
            slot_table[BLOCKS * P:, :].rearrange("(a n) o -> a (n o)", a=1), blank[0:1, 0:P]), tb, "table0")

        V.wait("iotas")
        V.do(lambda e: e.tensor_copy(iota_row[:, :], iota_row_i[:, :]))
        V.do(lambda e: e.tensor_copy(iota_col[:, :], iota_col_i[:, :]))
        V.do(lambda e: e.tensor_copy(kcol[:, :], kcol_i[:, :]))
        V.do(lambda e: e.tensor_copy(iota_chunk, junk.bitcast(I32)), "iota_f")
        V.wait("iota_f")
        V.do(lambda e: e.tensor_scalar(ident[:, :], iota_row[:, :], iota_col[:, :], None, ALU.is_equal))
        V.do(lambda e: e.tensor_scalar(before[:, :], iota_row[:, :], iota_col[:, :], None, ALU.is_gt))
        V.do(lambda e: e.memset(ones[:, :], 1.0), "consts")
        V.do(lambda e: e.tensor_scalar(row_ok[:, :], iota_col[:, :], float(LAST_ROWS), None, ALU.is_lt))
        V.do(lambda e: e.memset(tile_base[:, :, HEADS:AD], 1.0))
        V.do(lambda e: e.memset(neg_max[:, 0:1], -FAR_BELOW))
        V.do(lambda e: e.memset(run_max[:, 0:1], FAR_BELOW), "inits")

        V.wait("ends")
        V.do(lambda e: e.tensor_scalar(ends_i[:, :, :], ends_i[:, :, :], 7, None, ALU.arith_shift_right), "t0")
        V.wait("t0")
        V.do(lambda e: e.tensor_copy(row_a[:, :], ends_i[:, 0, :]))
        V.do(lambda e: e.tensor_copy(row_b[:, :], ends_i[:, 1, :]))
        V.do(lambda e: e.memset(row_d[:, :], 1.0), "t1")
        V.wait("t1")
        V.do(lambda e: e.scalar_tensor_tensor(row_b[:, :], row_b[:, :], 1.0, row_a[:, :], ALU.add,
                                              ALU.subtract), "t2")
        V.wait("t2")
        V.do(lambda e: e.tensor_tensor_scan(row_c[:, :], row_d[:, :], row_b[:, :], 0.0, ALU.mult, ALU.add),
             "t3")
        V.wait("t3")
        V.do(lambda e: e.tensor_tensor(row_c[:, :], row_c[:, :], row_b[:, :], ALU.subtract), "t4")
        V.wait("t4")
        V.do(lambda e: e.tensor_tensor(row_d[:, :], row_a[:, :], row_c[:, :], ALU.subtract), "t5")
        T.wait("consts", "t5")
        for n, row in enumerate((row_c, row_d)):
            for b in range(2):
                lo, hi = b * 512, min(CHUNKS, b * 512 + 512)
                T.do(lambda e, n=n, b=b, row=row, lo=lo, hi=hi: e.matmul(
                    bank[4 + 2 * n + b][:, 0:hi - lo], ones[0:1, :], row[:, lo:hi], start=True, stop=True),
                    ("chunk_bc", n, b))
        for n, to in enumerate((first_bc, delta_bc)):
            for b in range(2):
                lo, hi = b * 512, min(CHUNKS, b * 512 + 512)
                S.wait(("chunk_bc", n, b))
                S.do(copy_s(to[:, lo:hi], bank[4 + 2 * n + b][:, 0:hi - lo]), ("chunk_sb", n, b))
        def step_tables():
            V.wait(("chunk_sb", 1, 1))
            windows = [(max(0, b * P - (TILES - 1)), min(CHUNKS, (b + 1) * P)) for b in range(STEP_BLOCKS)]
            JUNKS = CHUNKS // (P + TILES - 1)

            def junk_of(b, width):
                at = b % JUNKS * (P + TILES - 1)
                return junk[:, at:at + width]
            for b, (lo, hi) in enumerate(windows):
                if b >= JUNKS:
                    V.wait(("count", b - JUNKS))
                V.do(lambda e, b=b, lo=lo, hi=hi: e.tensor_scalar(
                    junk_of(b, hi - lo), first_bc[:, lo:hi], kcol[:, b:b + 1], 0.0, ALU.is_le, ALU.add,
                    accum_out=step_c[:, b:b + 1]), ("count", b))
            for b, (lo, hi) in enumerate(windows):
                V.wait(("count", b))
                V.do(lambda e, b=b, lo=lo: e.tensor_scalar(step_c[:, b:b + 1], step_c[:, b:b + 1],
                                                           float(lo - 1), None, ALU.add), ("step_c", b))
            yield
            V.wait(("step_c", STEP_BLOCKS - 1))
            V.do(lambda e: e.tensor_copy(step_ci[:, :], step_c[:, :]), "step_ci")
            for b, (lo, hi) in enumerate(windows):
                if b >= JUNKS:
                    V.wait(("delta", b - JUNKS))
                V.do(lambda e, b=b, lo=lo, hi=hi: e.scalar_tensor_tensor(
                    junk_of(b, hi - lo), iota_chunk[:, lo:hi], step_c[:, b:b + 1], delta_bc[:, lo:hi],
                    ALU.is_equal, ALU.mult, accum_out=step_d[:, b:b + 1]), ("delta", b))
            yield
            V.wait(("delta", STEP_BLOCKS - 1))
            V.do(lambda e: e.tensor_tensor(step_t[:, :], step_d[:, :], kcol[:, :], ALU.add), "step_t")
            V.wait("step_t")
            V.do(lambda e: e.tensor_scalar(step_t128[:, :], step_t[:, :], float(P), None, ALU.mult))
            V.do(lambda e: e.tensor_scalar(step_tc[:, :], step_t[:, :], float(TILES - 1), None, ALU.min), "step_tc")
            T.wait("step_tc", ("chunk_sb", 1, 1))
            for n, col in enumerate((step_tc, step_t)):
                for b in range(STEP_BLOCKS):
                    T.do(lambda e, n=n, b=b, col=col: e.transpose(
                        bank[4 + 2 * n + b // 4][0:1, (b % 4) * P:(b % 4 + 1) * P], col[:, b:b + 1], ident[:, :]),
                        ("tile_tr", n, b))
            V.wait(("tile_tr", 0, STEP_BLOCKS - 1))
            V.do(lambda e: e.tensor_copy(tile_row[:, 0:512], bank[4][0:1, :]))
            V.do(lambda e: e.tensor_copy(tile_row[:, 512:STEP_BLOCKS * P], bank[5][0:1, 0:STEP_BLOCKS * P - 512]),
                 "tile_row")
            V.wait(("tile_tr", 1, STEP_BLOCKS - 1))
            half = 512 // GROUP
            V.do(lambda e: e.tensor_copy(tfirst[:, 0:half], bank[6][0:1, 0:512:GROUP]))
            V.do(lambda e: e.tensor_copy(tfirst[:, half:GROUPS], bank[7][0:1, 0:(GROUPS - half) * GROUP:GROUP]),
                 "tfirst")
            yield
            rows_d = [[counter(f"rows_dma{b}_{n}") for n in range(2)] for b in range(STEP_BLOCKS)]

            def fetch(b):
                if b == 0:
                    G.wait("step_ci", "src_pad", "dst_pad")
                for n, table in enumerate((src_pad, dst_pad)):
                    G.dma(lambda e, n=n, table=table: e.indirect_dma_start(
                        rows_i[:, 2 * b + n, :], None, table.rearrange("(c e) -> c e", e=P),
                        bass.IndirectOffsetOnAxis(step_ci[:, b:b + 1], 0)), rows_d[b][n], ("rows", b, n))
            for b in range(4):
                fetch(b)
                yield
            for b in range(STEP_BLOCKS):
                for n in range(2):
                    slot = 2 * (b % 2) + n
                    V.wait(("rows", b, n))
                    if b >= 2:
                        V.wait(("rows_tr", b - 2, n))
                    if n == 0:
                        V.do(lambda e, slot=slot, b=b, n=n: e.tensor_copy(rows_f[:, slot, :], rows_i[:, 2 * b + n, :]),
                             ("rows_f", b, n))
                    else:
                        V.do(lambda e, slot=slot, b=b, n=n: e.tensor_scalar(
                            rows_f[:, slot, :], rows_i[:, 2 * b + n, :], step_t128[:, b:b + 1], None, ALU.subtract),
                            ("rows_f", b, n))
                    T.wait(("rows_f", b, n))
                    if b >= 2:
                        T.wait(("rows_sb", b - 2, n))
                    elif b == 0:
                        T.wait("tfirst")
                    T.do(lambda e, slot=slot: e.transpose(bank[4 + slot][:, 0:P], rows_f[:, slot, :],
                                                          ident[:, :]), ("rows_tr", b, n))
                    w = min(P, STEPS - b * P)
                    to = (src_idx, dloc)[n][:, b * P:b * P + w]
                    S.wait(("rows_tr", b, n))
                    S.do(copy_s(to, bank[4 + slot][:, 0:w]), ("rows_sb", b, n))
                if b + 4 < STEP_BLOCKS:
                    fetch(b + 4)
                yield

        tmp_a = region2[:, 7 * 1024:7 * 1024 + F_IN]
        for c in range(KC):
            for n in range(2):
                V.wait("wg")
                V.do(lambda e, c=c, n=n: e.tensor_tensor(tmp_a, w_cat[:, c, 0:F_IN], a_bc[:, n, :], ALU.mult),
                     ("wa", c, n))
                V.wait(("wa", c, n))
                V.do(lambda e, c=c, n=n: e.tensor_reduce(
                    w_cat[:, c, F_IN + HEADS * n:F_IN + HEADS * (n + 1)],
                    tmp_a.rearrange("p (h o) -> p h o", o=F_OUT), AXIS_FREE, ALU.add), ("w_cat", c, n))
                V.wait(("w_cat", c, n))
        xn_buf = region2[:, 0:1024].rearrange("p (s f) -> p s f", f=F_IN)
        xt_buf = region2[:, 1024:2048].rearrange("p (s f) -> p s f", f=F_IN)
        s_buf = region2[:, 2048:3072].rearrange("p (s f) -> p s f", f=F_IN)
        h_buf = region2[:, 3072:3072 + 8 * ROW].rearrange("p (s c) -> p s c", c=ROW)
        h_out = [counter(f"h_out{i}") for i in range(2)]
        s_out = [counter(f"s_out{i}") for i in range(4)]

        def var_plus_eps(tag, t0, n):
            V.wait((tag, "aggr", t0 + n - 1))
            V.do(lambda e: e.tensor_scalar(var_eps[:, t0:t0 + n], mean_var[:, t0:t0 + n, 1], LN_EPS, None,
                                           ALU.add), (tag, "var_eps", t0))

        def root(tag, t0, n):
            S.wait((tag, "var_eps", t0))
            S.do(lambda e: e.activation(std[:, t0:t0 + n], var_eps[:, t0:t0 + n], ACT.Sqrt), (tag, "std", t0))

        def var_std(tag, t0, n):
            var_plus_eps(tag, t0, n)
            root(tag, t0, n)

        def inv_std(tag, t0, n, rstd=rstd):
            V.wait((tag, "std", t0))
            V.do(lambda e: e.reciprocal(rstd[:, t0:t0 + n], std[:, t0:t0 + n]), (tag, "rstd", t0))

        def many_stats(tag, t0, tile_ap):
            for t in range(t0, t0 + BATCH + 1):
                if t < t0 + BATCH:
                    V.do(lambda e, t=t: e.bn_stats(stats[:, t % BATCH, :], tile_ap(t)), (tag, "stats", t))
                if t > t0:
                    V.wait((tag, "stats", t - 1))
                    V.do(lambda e, t=t: e.bn_aggr(mean_var[:, t - 1, :], stats[:, (t - 1) % BATCH, :]),
                         (tag, "aggr", t - 1))

        H_GROUP = 4
        def a_stats(q):
            V.wait(("x", q))
            many_stats("A", q * BATCH, lambda t: x_all[:, t, :])
            var_std("A", q * BATCH, BATCH)

        a_stats(0)
        inv_std("A", 0, BATCH)
        T.wait(("w_cat", KC - 1, 1))
        tables = step_tables()
        blanked = 0
        for t in range(TILES):
            q, s4 = t // BATCH, t % 4
            next(tables, None)
            if t > TILES // 2 and t % 3 == 0 and blanked < TILES:
                n = min(7, TILES - blanked)
                if blanked == 0:
                    G.wait(("delta", STEP_BLOCKS - 1), "tfirst", "table0")
                G.do(lambda e, lo=blanked * ROW, hi=(blanked + n) * ROW: e.memset(acc[:, lo:hi], 0.0),
                     ("acc0", blanked))
                blanked += n
            if t % BATCH == 3 and q + 1 < BATCHES:
                a_stats(q + 1)
            if t % BATCH == 6 and q + 1 < BATCHES:
                inv_std("A", (q + 1) * BATCH, BATCH)
            if t >= 4:
                V.wait(("A_tr", t - 4), ("A_s", t - 4))
            V.wait(("A", "rstd", q * BATCH))
            V.do(lambda e, t=t, s4=s4: e.tensor_scalar(
                xn_buf[:, s4, :], x_all[:, t, :], mean_var[:, t, 0:1], rstd[:, t:t + 1], ALU.subtract,
                ALU.mult), ("A_xn", t))
            G.wait(("A_xn", t))
            if t >= 4:
                G.wait(("s_out", t - 4))
            G.do(lambda e, t=t, s4=s4: e.tensor_tensor(s_buf[:, s4, :], x_all[:, t, :], xn_buf[:, s4, :],
                                                       ALU.add), ("A_s", t))
            D.wait(("A_s", t))
            D.dma(lambda e, t=t, s4=s4: e.dma_start(x_plus_xn[t * P:(t + 1) * P, :], s_buf[:, s4, :]),
                  s_out[s4], ("s_out", t))
            T.wait(("A_xn", t))
            if t >= 2:
                T.wait(("A_xt", t - 2))
            for c in range(KC):
                T.do(lambda e, t=t, c=c, s4=s4: e.transpose(
                    bank[t % 2][:, c * P:(c + 1) * P], xn_buf[:, s4, c * P:(c + 1) * P], ident[:, :]),
                    ("A_tr", t) if c == KC - 1 else None)
            S.wait(("A_tr", t))
            if t >= 4:
                S.wait(("A_mm", t - 4))
            S.do(copy_s(xt_buf[:, s4, :], bank[t % 2][:, 0:F_IN]), ("A_xt", t))

            def a_matmul(t):
                s4 = t % 4
                T.wait(("A_xt", t))
                if t >= 2:
                    T.wait(("A_h", t - 2), ("A_ad", t - 2))
                for c in range(KC):
                    T.do(lambda e, t=t, c=c, s4=s4: e.matmul(
                        bank[2 + t % 2][:, 0:ROW + HEADS], xt_buf[:, s4, c * P:(c + 1) * P], w_cat[:, c, :],
                        start=(c == 0), stop=(c == KC - 1)), ("A_mm", t) if c == KC - 1 else None)
                s8 = t % 8
                S.wait(("A_mm", t))
                if t >= 8 and t % H_GROUP == 0:
                    S.wait(("h_out", t // H_GROUP - 2))
                S.do(copy_s(h_buf[:, s8, :], bank[2 + t % 2][:, 0:ROW]), ("A_h", t))
                S.do(copy_s(tile_base[:, t, 0:HEADS], bank[2 + t % 2][:, ROW:ROW + HEADS]), ("A_ad", t))
                if t % H_GROUP == H_GROUP - 1 or t == TILES - 1:
                    g = t // H_GROUP
                    n = t % H_GROUP + 1
                    D.wait(("A_h", t))
                    D.dma(lambda e, g=g, n=n: e.dma_start(
                        node_rows[g * H_GROUP * P:(g * H_GROUP + n) * P, :].rearrange("(t p) c -> p t c", p=P),
                        h_buf[:, (g % 2) * H_GROUP:(g % 2) * H_GROUP + n, :]), h_out[g % 2], ("h_out", g))
            if t >= 1:
                a_matmul(t - 1)
        a_matmul(TILES - 1)
        assert blanked == TILES and next(tables, "end") == "end"
        marks.put("acc0", *marks.at[("acc0", TILES - 7)])
        H_OUTS = (TILES - 1) // H_GROUP + 1

        T.wait("b1", ("A_h", TILES - 1), ("A_ad", TILES - 1))
        for f in range(FC):
            T.do(lambda e, f=f: e.transpose(bank[7][:, f * EXPERTS:(f + 1) * EXPERTS],
                                            b1_rows[:, f * P:(f + 1) * P], ident[0:EXPERTS, 0:EXPERTS]),
                 ("b1_tr", f))
        S.wait(("b1_tr", FC - 1))
        S.do(copy_s(b1_col[:, :, :].rearrange("p c e -> p (c e)"), bank[7][:, 0:FC * EXPERTS]), "b1_col")

        slot_at = [region2[:, i * GROUP * ROW:(i + 1) * GROUP * ROW] for i in range(3)]
        fourth = TILES * ROW + 8 * P
        slot_at.append(region1[:, fourth:fourth + GROUP * ROW])
        gathered = [v.rearrange("p (j c) -> p j c", c=ROW) for v in slot_at]
        SLOTS = len(gathered)
        row_in = [counter(f"row_in{i}") for i in range(SLOTS)]
        for g in range(GROUPS):
            if g == 0:
                for i in (H_OUTS - 2, H_OUTS - 1):
                    G.wait(("h_out", i))
                G.wait(("rows_sb", STEP_BLOCKS - 1, 0))
                for t in range(TILES - 4, TILES):
                    G.wait(("s_out", t))
                G.wait(("A_mm", TILES - 1))
            if g == SLOTS - 1:
                G.wait("b1_col")
            if g >= SLOTS:
                G.wait(("agg", g - SLOTS, GROUP - 1))
            for j in range(GROUP):
                k = g * GROUP + j
                G.dma(lambda e, g=g, j=j, k=k: e.indirect_dma_start(
                    gathered[g % SLOTS][:, j, :], None, node_rows,
                    bass.IndirectOffsetOnAxis(src_idx[:, k:k + 1], 0)), row_in[g % SLOTS],
                    ("row_in", g) if j == GROUP - 1 else None)

        TR_BANKS, Z_BANKS, M_BANK, AGG_BANKS = (0, 1), (2, 3), 4, (5, 6, 7)

        def b_onehot(g, js):
            if g >= GROUPS:
                return
            if g == 0:
                V.wait(("rows_sb", STEP_BLOCKS - 1, 1))
            if g >= 3:
                V.wait(("agg", g - 3, GROUP - 1))
            for j in js:
                k = g * GROUP + j
                V.do(lambda e, g=g, j=j, k=k: e.tensor_scalar(
                    onehot[:, (g % 3) * GROUP + j, :], iota_row[:, :], dloc[:, k:k + 1], None, ALU.is_equal),
                    ("onehot", g, j) if j % 4 == 3 else None)

        def b_transposes(g, halves=(0, 1)):
            for half in halves:
                T.wait(("onehot", g, half * 4 + 3))
                if g >= 1:
                    T.wait(("oh_t", g - 1, half))
                for j in range(half * 4, half * 4 + 4):
                    T.do(lambda e, g=g, j=j, half=half: e.transpose(
                        bank[TR_BANKS[half]][:, (j % 4) * P:(j % 4 + 1) * P],
                        onehot[:, (g % 3) * GROUP + j, :], ident[:, :]),
                        ("oh_tr", g, half) if j % 4 == 3 else None)
                S.wait(("oh_tr", g, half))
                if g >= 1:
                    S.wait(("ad_mm", g - 1))
                S.do(copy_s(onehot_t[:, half * 4:half * 4 + 4, :].rearrange("p s m -> p (s m)"),
                            bank[TR_BANKS[half]][:, :]), ("oh_t", g, half))

        def b_attn_dst(g):
            T.wait(("oh_t", g, 1))
            if g == 0:
                T.wait("tile_row", "inits", ("A_ad", TILES - 1))
            if g >= 2:
                T.wait(("z_add", g - 2), ("cap", g - 2))

            def emit(e, g=g):
                _, tiles = nc.values_load_multi_w_load_instructions(
                    tile_row[0:1, g * GROUP:(g + 1) * GROUP], engines=[mybir.EngineType.PE], min_val=0,
                    max_val=TILES - 1, skip_runtime_bounds_check_because="the value was clamped on chip")
                flat = tile_base[:, :, :].rearrange("p t c -> p (t c)")
                for j in range(GROUP):
                    ins = e.matmul(bank[Z_BANKS[g % 2]][:, j * AD:(j + 1) * AD], onehot_t[:, j, :],
                                   flat[:, bass.ds(tiles[j] * AD, AD)], start=True, stop=True)
                return ins
            T.do(emit, ("ad_mm", g))
            S.wait(("ad_mm", g))
            if g >= 2:
                S.wait(("z_cap", g - 2))
            S.do(lambda e, g=g: e.activation(
                cap[:, g % 2, :],
                bank[Z_BANKS[g % 2]][:, 0:GROUP * AD].rearrange("p (j c) -> p j c", c=AD)[:, :, HEADS],
                ACT.Copy, bias=FAR_BELOW, scale=-2.0 * FAR_BELOW), ("cap", g))

        def b_logits(g):
            zg = z[:, g % 2, :, :]
            V.wait(("row_in", g), ("cap", g))
            if g >= 2:
                V.wait(("p", g - 2))
            V.do(lambda e: e.tensor_tensor(
                zg, bank[Z_BANKS[g % 2]][:, 0:GROUP * AD].rearrange("p (j c) -> p j c", c=AD)[:, :, 0:HEADS],
                gathered[g % SLOTS][:, :, F_IN:ROW], ALU.add), ("z_add", g))
            b_onehot(g + 1, (0,))
            V.wait(("z_add", g))
            V.do(lambda e: e.scalar_tensor_tensor(zg, zg, SLOPE, zg, ALU.mult, ALU.max), ("z_relu", g))
            b_onehot(g + 1, (1,))
            V.wait(("z_relu", g), ("cap", g))
            V.do(lambda e: e.tensor_tensor(zg, zg, cap[:, g % 2, :].unsqueeze(2).broadcast_to(
                [P, GROUP, HEADS]), ALU.min), ("z_cap", g))
            b_onehot(g + 1, (2,))
            V.wait(("z_cap", g))
            if g >= 2:
                V.wait(("max_tr", g - 2))
            V.do(lambda e: e.tensor_reduce(zmax[:, g % 2:g % 2 + 1], zg.rearrange("p j h -> p (j h)"),
                                           AXIS_FREE, ALU.max), ("zmax", g))
            b_onehot(g + 1, (3,))

        def b_max_tr(g):
            T.wait(("zmax", g))
            if g >= 1:
                T.wait(("gmax", g - 1))
            T.do(lambda e: e.transpose(bank[M_BANK][0:1, 0:P], zmax[:, g % 2:g % 2 + 1], ident[:, :]),
                 ("max_tr", g))

        def b_max(g):
            V.wait(("max_tr", g))
            V.do(lambda e: e.tensor_reduce(gmax[:, g % 2:g % 2 + 1], bank[M_BANK][0:1, 0:P], AXIS_FREE,
                                           ALU.max), ("gmax", g))
            V.wait(("gmax", g))
            V.do(lambda e: e.tensor_tensor(run_max[:, g + 1:g + 2], run_max[:, g:g + 1],
                                           gmax[:, g % 2:g % 2 + 1], ALU.max), ("run_max", g))

        def b_max_bc(g):
            T.wait(("run_max", g))
            if g >= 1:
                T.wait(("neg_max", g - 1))
            T.do(lambda e: e.matmul(bank[M_BANK][:, P + 8:P + 9], ones[0:1, :], run_max[:, g + 1:g + 2],
                                    start=True, stop=True), ("max_bc", g))

        def b_exp(g):
            S.wait(("max_bc", g))
            S.do(lambda e: e.activation(neg_max[:, g + 1:g + 2], bank[M_BANK][:, P + 8:P + 9], ACT.Copy,
                                        scale=-1.0), ("neg_max", g))
            S.wait(("neg_max", g), ("z_cap", g))
            S.do(lambda e: e.activation(gathered[g % SLOTS][:, :, F_IN:ROW], z[:, g % 2, :, :], ACT.Exp,
                                        bias=neg_max[:, g + 1:g + 2]), ("p", g))
            S.do(lambda e: e.activation(fall[:, g:g + 1], neg_max[:, g:g + 1], ACT.Exp, scale=-1.0,
                                        bias=neg_max[:, g + 1:g + 2]), ("fall", g))

        def b_weigh(g, quarter):
            V.wait(("p", g))
            js = slice(quarter * 2, quarter * 2 + 2)
            hv = gathered[g % SLOTS][:, js, 0:F_IN].rearrange("p j (h o) -> p j h o", o=F_OUT)
            pv = gathered[g % SLOTS][:, js, F_IN:ROW].unsqueeze(3).broadcast_to([P, 2, HEADS, F_OUT])
            V.do(lambda e: e.tensor_tensor(hv, hv, pv, ALU.mult), ("weigh", g, quarter))

        def b_aggregate(g, js):
            for j in js:
                k = g * GROUP + j
                T.wait(("weigh", g, j // 2))
                if k >= 3:
                    T.wait(("add", (k - 3) // GROUP, (k - 3) % GROUP))
                T.do(lambda e, g=g, j=j, k=k: e.matmul(
                    bank[AGG_BANKS[k % 3]][:, 0:ROW], onehot[:, (g % 3) * GROUP + j, :],
                    gathered[g % SLOTS][:, j, :], start=True, stop=True), ("agg", g, j))

        add_tiles = {}

        def b_add_tiles(g):
            def load(e):
                _, add_tiles[g] = nc.values_load_multi_w_load_instructions(
                    tile_row[0:1, g * GROUP:(g + 1) * GROUP], engines=[mybir.EngineType.DVE], min_val=0,
                    max_val=TILES - 1, skip_runtime_bounds_check_because="the value was clamped on chip")
            if g == 0:
                V.wait("acc0", "tile_row")
            V.do(load)

        def b_add(g, j):
            k = g * GROUP + j
            if j == 0:
                V.wait(("fall", g))
            V.wait(("agg", g, j))
            if k >= 1:
                V.wait(("add", (k - 1) // GROUP, (k - 1) % GROUP))

            def emit(e):
                rows = acc[:, bass.ds(add_tiles[g][j] * ROW, ROW)]
                new = bank[AGG_BANKS[k % 3]][:, 0:ROW]
                if j == 0:
                    return e.scalar_tensor_tensor(rows, rows, fall[:, g:g + 1], new, ALU.mult, ALU.add)
                return e.tensor_tensor(rows, rows, new, ALU.add)
            V.do(emit, ("add", g, j))

        w1_ld = counter("ld_w1")

        def load_w1(part):
            e0, c = part // KC * 4, part % KC
            if part == 0:
                D.wait(("A_xn", TILES - 1), ("A_s", TILES - 1))
            D.dma(lambda e: e.dma_start(
                w1_sb.rearrange("p (x c f) -> p x c f", c=KC, f=HIDDEN)[:, e0:e0 + 4, c, :],
                w1[e0:e0 + 4, c * P:(c + 1) * P, :].rearrange("x p f -> p x f")), w1_ld,
                "w1" if e0 + 4 == EXPERTS and c == KC - 1 else None)

        b_onehot(0, range(GROUP))
        b_transposes(0)
        b_attn_dst(0)
        for g in range(GROUPS + 1):
            now, last, more = g < GROUPS, g >= 1, g + 1 < GROUPS
            if last:
                b_add_tiles(g - 1)
            if now:
                b_logits(g)
            for j in range(GROUP):
                if last:
                    b_add(g - 1, j)
                if j < 4:
                    b_onehot(g + 1, (4 + j,))
                if now and j == 1:
                    b_max(g)
                if now and j >= 4:
                    b_weigh(g, j - 4)
            if last:
                b_aggregate(g - 1, range(0, 3))
            if now:
                b_max_tr(g)
            if last:
                b_aggregate(g - 1, range(3, 5))
            if now:
                b_max_bc(g)
                b_exp(g)
            if more:
                b_transposes(g + 1, (0,))
            if last:
                b_aggregate(g - 1, range(5, 6))
            if more:
                b_transposes(g + 1, (1,))
            if last:
                b_aggregate(g - 1, range(6, GROUP))
            if more:
                b_attn_dst(g + 1)
            if g % 8 == 7 and g // 8 < EXPERTS // 4 * KC:
                D.wait(("agg", g - 1, GROUP - 1))
                load_w1(g // 8)

        LAST = ("add", GROUPS - 1, GROUP - 1)
        T.wait("tfirst", LAST)
        T.do(lambda e: e.matmul(bank[0][:, 0:GROUPS], ones[0:1, :], tfirst[:, :], start=True, stop=True),
             "tfirst_bc")
        V.wait("tfirst_bc", ("neg_max", GROUPS - 1))
        V.do(lambda e: e.tensor_scalar(late[:, :], bank[0][:, 0:GROUPS], iota_col[:, :], -FAR_BELOW,
                                       ALU.is_gt, ALU.mult), "late")
        V.wait("late")
        V.do(lambda e: e.tensor_tensor(late[:, :], late[:, :], neg_max[:, 1:GROUPS + 1], ALU.add), "late2")
        V.wait("late2")
        V.do(lambda e: e.tensor_reduce(late_min[:, :], late[:, :], AXIS_FREE, ALU.min), "late_min")
        V.wait("late_min")
        V.do(lambda e: e.tensor_scalar(late_min[:, :], late_min[:, :], neg_max[:, GROUPS:GROUPS + 1], EXP_TOP,
                                       ALU.subtract, ALU.min), "late3")
        S.wait("late3")
        S.do(lambda e: e.activation(late_min[:, :], late_min[:, :], ACT.Exp), "late4")
        T.wait("late4", "late")
        T.do(lambda e: e.transpose(bank[0][0:1, 0:P], late_min[:, :], ident[:, :]), "eps_tr")
        V.wait("eps_tr")
        V.do(lambda e: e.tensor_scalar(eps_row[:, :], bank[0][0:1, 0:P], SUM_EPS, None, ALU.mult), "eps_row")
        T.wait("eps_row")
        T.do(lambda e: e.matmul(bank[1][:, 0:TILES], ones[0:1, :], eps_row[:, 0:TILES], start=True, stop=True),
             "eps_bc")
        V.wait("eps_bc")
        V.do(lambda e: e.tensor_copy(eps_bc[:, :], bank[1][:, 0:TILES]), "eps")
        V.do(lambda e: e.tensor_scalar(base[:, 0, :], iota_row[:, 0:EXPERTS], float(TILES * P), None, ALU.mult),
             "base0")

        s_all = region2[:, 0:2 * BATCH * F_IN].rearrange("p (s t f) -> p s t f", s=2, f=F_IN)
        y_all = region2[:, 2 * BATCH * F_IN:4 * BATCH * F_IN].rearrange("p (s t f) -> p s t f", s=2, f=F_IN)
        yt_buf = region2[:, 4 * BATCH * F_IN:4 * BATCH * F_IN + 2 * F_IN].rearrange("p (s f) -> p s f", f=F_IN)
        s_in = [counter(f"s_in{i}") for i in range(2)]
        y_out = [counter(f"y_out{i}") for i in range(2)]
        x1_out = [counter(f"x1_out{i}") for i in range(2)]
        table_dma = counter("table_dma")
        w2_ld = counter("ld_w2")
        w2_at = 0

        def rows_of(table, q):
            return table[q * BATCH * P:(q + 1) * BATCH * P, :].rearrange("(t p) f -> p t f", p=P)

        def c_load(q):
            if q < 2:
                D.wait(("agg", GROUPS - 4 + q, GROUP - 1))
            else:
                D.wait(("x1_out", q - 2), ("C_y0", (q - 1) * BATCH - 1))
            D.dma(lambda e: e.dma_start(s_all[:, q % 2, :, :], rows_of(x_plus_xn, q)), s_in[q % 2], ("s_in", q))

        def c_residual(q):
            t0 = q * BATCH
            hv = acc_t[:, t0:t0 + BATCH, 0:F_IN].rearrange("p t (h o) -> p t h o", o=F_OUT)
            if q == 0:
                V.wait("eps", LAST)
            sums = rsum[:, t0:t0 + BATCH, :]
            V.do(lambda e: e.tensor_tensor(
                sums, acc_t[:, t0:t0 + BATCH, F_IN:ROW],
                eps_bc[:, t0:t0 + BATCH].unsqueeze(2).broadcast_to([P, BATCH, HEADS]), ALU.add), ("C_sums", q))
            V.wait(("C_sums", q))
            V.do(lambda e: e.reciprocal(sums, sums), ("C_rsum", q))
            V.wait(("C_rsum", q))
            V.do(lambda e: e.tensor_tensor(
                hv, hv, rsum[:, t0:t0 + BATCH, :].unsqueeze(3).broadcast_to([P, BATCH, HEADS, F_OUT]),
                ALU.mult), ("C_gat", q))
            V.wait(("C_gat", q), ("s_in", q))
            V.do(lambda e: e.tensor_tensor(s_all[:, q % 2, :, :], acc_t[:, t0:t0 + BATCH, 0:F_IN],
                                           s_all[:, q % 2, :, :], ALU.add), ("C_x1", q))
            D.wait(("C_x1", q))
            D.dma(lambda e: e.dma_start(rows_of(x1_rows, q), s_all[:, q % 2, :, :]), x1_out[q % 2],
                  ("x1_out", q))
            V.wait(("C_x1", q))
            many_stats("C", t0, lambda t: s_all[:, q % 2, t % BATCH, :])
            var_std("C", t0, BATCH)

        def c_shift(q):
            t0 = q * BATCH
            inv_std("C", t0, BATCH)
            V.wait(("C", "rstd", t0))
            V.do(lambda e: e.scalar_tensor_tensor(shift[:, t0:t0 + BATCH], mean_var[:, t0:t0 + BATCH, 0], -1.0,
                                                  rstd[:, t0:t0 + BATCH], ALU.mult, ALU.mult), ("C_shift", q))

        def c_gate(t):
            q = t // BATCH
            S.wait(("C_ytr", t))
            if t >= 2:
                S.wait(("C_gate", t - 2))
            S.do(copy_s(yt_buf[:, t % 2, :], bank[4 + t % 2][:, 0:F_IN]), ("C_yt", t))
            T.wait(("C_yt", t))
            if q >= 2:
                T.wait(("C_logits", q - 2))
            lg = bank[2 + q % 2][:, (t % BATCH) * EXPERTS:(t % BATCH + 1) * EXPERTS]
            for c in range(KC):
                T.do(lambda e, t=t, c=c, lg=lg: e.matmul(lg, yt_buf[:, t % 2, c * P:(c + 1) * P],
                                                         gate_sb[:, c, :], start=(c == 0), stop=(c == KC - 1)),
                     ("C_gate", t) if c == KC - 1 else None)

        def c_norm(q):
            t0 = q * BATCH
            for t in range(t0, t0 + BATCH):
                S.wait(("C_shift", q))
                if q >= 2:
                    S.wait(("y_out", q - 2))
                S.do(lambda e, t=t: e.activation(y_all[:, q % 2, t % BATCH, :], s_all[:, q % 2, t % BATCH, :],
                                                 ACT.Identity, bias=shift[:, t:t + 1], scale=rstd[:, t:t + 1]),
                     ("C_y0", t))
                T.wait(("C_y0", t))
                if t == 0:
                    T.wait("gate")
                if t >= 2:
                    T.wait(("C_yt", t - 2))
                for c in range(KC):
                    T.do(lambda e, t=t, c=c: e.transpose(
                        bank[4 + t % 2][:, c * P:(c + 1) * P],
                        y_all[:, q % 2, t % BATCH, c * P:(c + 1) * P], ident[:, :]),
                        ("C_ytr", t) if c == KC - 1 else None)
                if t > t0:
                    c_gate(t - 1)
            c_gate(t0 + BATCH - 1)
            D.wait(("C_y0", t0 + BATCH - 1))
            D.dma(lambda e: e.dma_start(rows_of(y0_rows, q), y_all[:, q % 2, :, :]), y_out[q % 2], ("y_out", q))

        def c_choose(q):
            t0 = q * BATCH
            V.wait(("C_gate", t0 + BATCH - 1))
            V.do(lambda e: e.tensor_tensor(
                logits[:, t0:t0 + BATCH, :],
                bank[2 + q % 2][:, 0:BATCH * EXPERTS].rearrange("p (t e) -> p t e", e=EXPERTS),
                gate_b_bc[:, :].unsqueeze(1).broadcast_to([P, BATCH, EXPERTS]), ALU.add), ("C_logits", q))
            V.wait(("C_logits", q))
            for t in range(t0, t0 + BATCH):
                V.do(lambda e, t=t: e.max(top_v[:, t, :], logits[:, t, :]), ("C_top", t))
            for t in range(t0, t0 + BATCH):
                V.wait(("C_top", t))
                V.do(lambda e, t=t: e.max_index(top_i[:, t, :], top_v[:, t, :], logits[:, t, :]), ("C_idx", t))
            V.wait(("C_idx", t0 + BATCH - 1))
            V.do(lambda e: e.tensor_copy(top_f[:, :, :], top_i[:, t0:t0 + BATCH, 0:TOP_K]), ("C_topf", q))
            V.wait(("C_topf", q))
            if q >= 1:
                V.wait(("C_tot", q - 1), ("C_pos", q - 1))
            for k in range(TOP_K):
                V.do(lambda e, k=k: e.tensor_tensor(
                    chosen[:, k, :, :], iota_row[:, 0:EXPERTS].unsqueeze(1).broadcast_to([P, BATCH, EXPERTS]),
                    top_f[:, :, k:k + 1].broadcast_to([P, BATCH, EXPERTS]), ALU.is_equal), ("C_ch", q, k))
            V.wait(("C_ch", q, 1))
            V.do(lambda e: e.tensor_tensor(both[:, :, :], chosen[:, 0, :, :], chosen[:, 1, :, :], ALU.add),
                 ("C_both0", q))
            V.wait(("C_both0", q))
            if q == BATCHES - 1:
                V.do(lambda e: e.tensor_scalar(both[:, BATCH - 1, :], both[:, BATCH - 1, :], row_ok[:, :], None,
                                               ALU.mult), ("C_both", q))
            else:
                marks.put(("C_both", q), *marks.at[("C_both0", q)])
            T.wait(("C_both", q))
            if q >= 1:
                T.wait(("C_rank", q - 1), ("C_base", t0 - 1))
            flat = both[:, :, :].rearrange("p t e -> p (t e)")
            T.do(lambda e: e.matmul(bank[7][:, 0:BATCH * EXPERTS], ones[:, :], flat, start=True, stop=True),
                 ("C_tot", q))
            T.do(lambda e: e.matmul(bank[6][:, 0:BATCH * EXPERTS], before[:, :], flat, start=True, stop=True),
                 ("C_bef", q))

        def c_slots(q):
            t0 = q * BATCH
            V.wait(("C_tot", q), "base0")
            for t in range(t0, t0 + BATCH):
                if t > 0:
                    V.wait(("C_base", t - 1))
                o = (t - t0) * EXPERTS
                V.do(lambda e, t=t, o=o: e.tensor_tensor(base[:, t + 1, :], base[:, t, :],
                                                         bank[7][:, o:o + EXPERTS], ALU.add), ("C_base", t))
            V.wait(("C_base", t0 + BATCH - 1), ("C_bef", q))
            V.do(lambda e: e.tensor_tensor(rank[:, :, :], base[:, t0:t0 + BATCH, :],
                                           bank[6][:, 0:BATCH * EXPERTS].rearrange("p (t e) -> p t e",
                                                                                   e=EXPERTS), ALU.add),
                 ("C_rank", q))
            V.wait(("C_rank", q))
            V.do(lambda e: e.tensor_tensor(picked[:, :, :, :], chosen[:, :, :, :],
                                           rank[:, :, :].unsqueeze(1).broadcast_to([P, TOP_K, BATCH, EXPERTS]),
                                           ALU.mult), ("C_pick", q))
            V.wait(("C_pick", q))
            V.do(lambda e: e.tensor_reduce(pos_f[:, :, :], picked[:, :, :, :], AXIS_FREE, ALU.add),
                 ("C_posf", q))
            V.wait(("C_posf", q))
            V.do(lambda e: e.tensor_copy(pos_i[:, :, t0:t0 + BATCH], pos_f[:, :, :]), ("C_pos", q))

        def c_scatter(q):
            G.wait(("C_pos", q), "table0", "dest")
            for t in range(q * BATCH, (q + 1) * BATCH):
                rows = P if t < TILES - 1 else LAST_ROWS
                for k in range(TOP_K):
                    G.dma(lambda e, t=t, k=k, rows=rows: e.indirect_dma_start(
                        slot_table, bass.IndirectOffsetOnAxis(pos_i[0:rows, k, t:t + 1], 0),
                        dest_i[0:rows, t, k:k + 1], None), table_dma,
                        ("table", t) if k == TOP_K - 1 else None)

        def c_w2(q):
            nonlocal w2_at
            done = BATCH * (q + 1)
            while w2_at < EXPERTS and ((w2_at + 1) * FC * F_IN <= done * ROW or done == TILES):
                x_ = w2_at
                D.dma(lambda e, x_=x_: e.dma_start(
                    w2_sb.rearrange("p (x c f) -> p x c f", c=FC, f=F_IN)[:, x_, :, :],
                    w2[x_, :, :].rearrange("(c p) f -> p c f", p=P)), w2_ld,
                    "w2" if x_ == EXPERTS - 1 else None)
                w2_at += 1

        c_load(0)
        c_load(1)
        c_residual(0)
        c_shift(0)
        c_norm(0)
        for q in range(BATCHES):
            if q + 1 < BATCHES:
                c_residual(q + 1)
                if q + 2 < BATCHES:
                    c_load(q + 2)
            c_choose(q)
            if q + 1 < BATCHES:
                c_shift(q + 1)
            c_slots(q)
            c_scatter(q)
            if q + 1 < BATCHES:
                c_norm(q + 1)
            c_w2(q)
        b2_ld = counter("ld_b2")
        D.wait("gap", "d0")
        D.dma(lambda e: e.dma_start(b2_bc, b2.rearrange("x f -> (x f)").partition_broadcast(P)), b2_ld, "b2")

        V.wait(("C_top", TILES - 1))
        V.do(lambda e: e.tensor_tensor(gap[:, :], top_v[:, :, 1], top_v[:, :, 0], ALU.subtract), "gap")
        S.wait("gap")
        S.do(lambda e: e.activation(weight[:, 1, :], gap[:, :], ACT.Exp), "gap_exp")
        V.wait("gap_exp")
        V.do(lambda e: e.tensor_scalar(gap[:, :], weight[:, 1, :], 1.0, None, ALU.add), "gap1")
        V.wait("gap1")
        V.do(lambda e: e.reciprocal(weight[:, 0, :], gap[:, :]), "weight0")
        V.wait("weight0")
        V.do(lambda e: e.tensor_tensor(weight[:, 1, :], weight[:, 1, :], weight[:, 0, :], ALU.mult), "weight1")

        V.wait(("C_base", TILES - 1))
        V.do(lambda e: e.tensor_tensor(cnt_f[:, :], base[:, TILES, :], base[:, 0, :], ALU.subtract), "d0")
        V.wait("d0")
        V.do(lambda e: e.tensor_scalar(cnt_f[:, :], cnt_f[:, :], float(P - 1), None, ALU.add), "d1")
        V.wait("d1")
        V.do(lambda e: e.tensor_copy(cnt_i[:, :], cnt_f[:, :]), "d2")
        V.wait("d2")
        V.do(lambda e: e.tensor_scalar(cnt_i[:, :], cnt_i[:, :], 7, None, ALU.arith_shift_right), "d3")
        V.wait("d3")
        V.do(lambda e: e.tensor_copy(ntile[:, :], cnt_i[:, :]), "d4")
        V.wait("d4")
        V.do(lambda e: e.tensor_tensor_scan(incl[:, :], ones[:, 0:EXPERTS], ntile[:, :], 0.0, ALU.mult,
                                            ALU.add), "d5")
        V.wait("d5")
        V.do(lambda e: e.tensor_tensor(excl[:, :], incl[:, :], ntile[:, :], ALU.subtract), "d6")
        V.do(lambda e: e.tensor_scalar(smalls[:, :], incl[:, :], iota_col[:, :], 0.0, ALU.is_le, ALU.add,
                                       accum_out=small[:, 0:1]), "d7")
        V.wait("d7", "d6")
        V.do(lambda e: e.scalar_tensor_tensor(smalls[:, :], iota_row[:, 0:EXPERTS], small[:, 0:1], excl[:, :],
                                              ALU.is_equal, ALU.mult, accum_out=small[:, 1:2]), "d8")
        V.wait("d8")
        V.do(lambda e: e.tensor_tensor(small[:, 2:3], iota_col[:, :], small[:, 1:2], ALU.subtract), "d9")
        V.wait("d9")
        V.do(lambda e: e.scalar_tensor_tensor(small[:, 3:4], small[:, 0:1], float(TILES), small[:, 2:3],
                                              ALU.mult, ALU.add), "d10")
        V.wait("d10")
        V.do(lambda e: e.tensor_scalar(small[:, 4:5], small[:, 3:4], float(BLOCKS), None, ALU.min), "d11")
        V.do(lambda e: e.tensor_scalar(small[:, 5:6], small[:, 0:1], float(EXPERTS - 1), None, ALU.min), "d12")
        V.wait("d11")
        V.do(lambda e: e.tensor_copy(blk_i[:, :], small[:, 4:5]), "blk")
        slots_d = counter("slots_dma")
        G.wait("blk", ("table", TILES - 1))
        G.dma(lambda e: e.indirect_dma_start(slots_i[:, :], None, slot_table.rearrange("(b s) o -> b (s o)", s=P),
                                             bass.IndirectOffsetOnAxis(blk_i[:, :], 0)), slots_d, "slots")
        T.wait("d12", "eps")
        T.do(lambda e: e.transpose(bank[0][0:1, 0:P], small[:, 5:6], ident[:, :]), "ex_tr")
        V.wait("ex_tr")
        V.do(lambda e: e.tensor_copy(expert_row[:, :], bank[0][0:1, 0:P]), "expert_row")
        V.wait("slots")
        V.do(lambda e: e.tensor_copy(slots_f[:, :], slots_i[:, :]), "slots_f")
        T.wait("slots_f")
        T.do(lambda e: e.transpose(bank[1][:, 0:P], slots_f[:, :], ident[:, :]), "slots_tr")
        V.wait("slots_tr")
        V.do(lambda e: e.tensor_copy(dest_u[:, :], bank[1][:, 0:P]), "dest_u")
        V.wait("dest_u")
        V.do(lambda e: e.tensor_scalar(token_u[:, :], dest_u[:, :], 1, None, ALU.logical_shift_right), "tok0")
        V.wait("tok0")
        V.do(lambda e: e.tensor_scalar(token_u[:, :], token_u[:, :], float(NODES - 1), None, ALU.min), "token")

        XG = 4
        at = 0

        def take(n, w):
            nonlocal at
            v = region2[:, at:at + n * w].rearrange("p (s f) -> p s f", f=w)
            at += n * w
            return v
        xg_buf, xgt_buf = take(XG, F_IN), take(2, F_IN)
        w1_buf, hidt_buf, y_buf = take(2, KC * HIDDEN), take(2, HIDDEN), take(3, F_IN)
        xg_in = [counter(f"xg_in{i}") for i in range(XG)]
        yb_out = [counter(f"yb_out{i}") for i in range(3)]
        flat_w1 = w1_sb
        flat_w2 = w2_sb

        def d_gather(j):
            if j == 0:
                G.wait("token")
                for q in (BATCHES - 2, BATCHES - 1):
                    G.wait(("y_out", q), ("x1_out", q))
            if j >= XG:
                G.wait(("D_xtr", j - XG))
            G.dma(lambda e: e.indirect_dma_start(xg_buf[:, j % XG, :], None, y0_rows,
                                                 bass.IndirectOffsetOnAxis(token_u[:, j:j + 1], 0)),
                  xg_in[j % XG], ("xg", j))

        def d_scatter(j):
            G.wait(("D_y", j))
            G.dma(lambda e: e.indirect_dma_start(
                choice_rows, bass.IndirectOffsetOnAxis(dest_u[:, j:j + 1], 0), y_buf[:, j % 3, :], None,
                bounds_check=NODES * TOP_K - 1, oob_is_err=False), yb_out[j % 3], ("yb_out", j))

        X_BANKS, HIDT_BANKS, Y_BANKS = (0, 1), (2, 3), (6, 7)

        def d_xtr(j):
            T.wait(("xg", j))
            if j == 0:
                T.wait("dest_u", "expert_row")
            if j >= 2:
                T.wait(("D_xt", j - 2))
            for c in range(KC):
                T.do(lambda e, c=c: e.transpose(bank[X_BANKS[j % 2]][:, c * P:(c + 1) * P],
                                                xg_buf[:, j % XG, c * P:(c + 1) * P], ident[:, :]),
                     ("D_xtr", j) if c == KC - 1 else None)
            V.wait(("D_xtr", j))
            if j >= 2:
                V.wait(("D_l1", j - 2))
            V.do(lambda e: e.tensor_copy(xgt_buf[:, j % 2, :], bank[X_BANKS[j % 2]][:, 0:F_IN]), ("D_xt", j))

        experts = {}

        def load_experts(queue, use, j):
            if j % GROUP == 0:
                n = min(GROUP, SLOT_TILES - j)

                def load(e):
                    _, experts[use] = nc.values_load_multi_w_load_instructions(
                        expert_row[0:1, j:j + n], engines=[e.engine], min_val=0, max_val=EXPERTS - 1,
                        skip_runtime_bounds_check_because="the value was clamped on chip")
                if j == 0:
                    queue.wait("expert_row")
                queue.do(load)

        def d_weights(j):
            if j == 0:
                V.wait("w1")
            if j >= 2:
                V.wait(("D_l1", j - 2))
            load_experts(V, "weights", j)

            def emit(e):
                x_ = experts["weights"][j % GROUP]
                return e.tensor_copy(w1_buf[:, j % 2, :],
                                     flat_w1[:, bass.ds(x_ * (KC * HIDDEN), KC * HIDDEN)])
            V.do(emit, ("D_w1", j))

        def d_layer1(j):
            T.wait(("D_xt", j), ("D_w1", j))
            if j >= 2:
                T.wait(("D_ht", j - 2))
            for f in range(FC):
                for c in range(KC):
                    T.do(lambda e, f=f, c=c: e.matmul(
                        bank[HIDT_BANKS[j % 2]][:, f * P:(f + 1) * P],
                        w1_buf[:, j % 2, c * HIDDEN + f * P:c * HIDDEN + (f + 1) * P],
                        xgt_buf[:, j % 2, c * P:(c + 1) * P], start=(c == 0), stop=(c == KC - 1)),
                        ("D_l1", j) if f == FC - 1 and c == KC - 1 else None)
            S.wait(("D_l1", j))
            if j == 0:
                S.wait("b1_col")
            if j >= 2:
                S.wait(("D_l2", j - 2))

            load_experts(S, "b1", j)

            def emit_s(e):
                x_ = experts["b1"][j % GROUP]
                flat_b1 = b1_col[:, :, :].rearrange("p c e -> p (c e)")
                for f in range(FC):
                    ins = e.activation(hidt_buf[:, j % 2, f * P:(f + 1) * P],
                                       bank[HIDT_BANKS[j % 2]][:, f * P:(f + 1) * P], ACT.Relu,
                                       bias=flat_b1[:, bass.ds(x_ + f * EXPERTS, 1)])
                return ins
            S.do(emit_s, ("D_ht", j))

        def d_layer2(j):
            T.wait(("D_ht", j))
            if j == 0:
                T.wait("w2")
            if j >= 2:
                T.wait(("D_y", j - 2))

            load_experts(T, "w2", j)

            def emit(e):
                x_ = experts["w2"][j % GROUP]
                for f in range(FC):
                    ins = e.matmul(bank[Y_BANKS[j % 2]][:, 0:F_IN], hidt_buf[:, j % 2, f * P:(f + 1) * P],
                                   flat_w2[:, bass.ds(x_ * (FC * F_IN) + f * F_IN, F_IN)],
                                   start=(f == 0), stop=(f == FC - 1))
                return ins
            T.do(emit, ("D_l2", j))
            V.wait(("D_l2", j))
            if j == 0:
                V.wait("b2")
            if j >= 3:
                V.wait(("yb_out", j - 3))

            load_experts(V, "b2", j)

            def emit_y(e):
                x_ = experts["b2"][j % GROUP]
                return e.tensor_tensor(y_buf[:, j % 3, :], bank[Y_BANKS[j % 2]][:, 0:F_IN],
                                       b2_bc[:, bass.ds(x_ * F_IN, F_IN)], ALU.add)
            V.do(emit_y, ("D_y", j))

        for j in range(XG - 1):
            d_gather(j)
        for j in range(2):
            d_xtr(j)
            d_weights(j)
        for i in range(SLOT_TILES + 1):
            if i < SLOT_TILES:
                d_layer1(i)
            if i + 2 < SLOT_TILES:
                d_xtr(i + 2)
                d_weights(i + 2)
            if i >= 1:
                d_layer2(i - 1)
            if i + XG - 1 < SLOT_TILES:
                d_gather(i + XG - 1)
            if i >= 1:
                d_scatter(i - 1)

        E_TILES = (3, 6, 7, 7, 7, 7, 7, 3, 2)
        assert sum(E_TILES) == TILES and max(E_TILES) <= BATCH
        e_first = [sum(E_TILES[:i]) for i in range(len(E_TILES))]
        E_SLOTS = 4
        n_e = BATCH * F_IN
        e_slot = [r[:, h * 4 * n_e:(h + 1) * 4 * n_e] for r in (region0, region1) for h in range(2)]
        e_x1 = [v[:, 0:n_e].rearrange("p (t f) -> p t f", f=F_IN) for v in e_slot]
        e_y = [v[:, n_e:2 * n_e].rearrange("p (t f) -> p t f", f=F_IN) for v in e_slot]
        e_ch = [v[:, 2 * n_e:4 * n_e].rearrange("p (t k f) -> p t k f", k=TOP_K, f=F_IN) for v in e_slot]
        e_x1in = [counter(f"e_x1in{i}") for i in range(E_SLOTS)]
        e_chin = [counter(f"e_chin{i}") for i in range(E_SLOTS)]
        out_d = [counter(f"out{i}") for i in range(E_SLOTS)]

        def e_load_x1(i):
            t0, n, s = e_first[i], E_TILES[i], i % E_SLOTS
            if i == 0:
                D.wait(("D_w1", SLOT_TILES - 1))
            if i == 2:
                D.wait(("D_l2", SLOT_TILES - 1))
            if i >= E_SLOTS:
                D.wait(("out", i - E_SLOTS))
            D.dma(lambda e: e.dma_start(e_x1[s][:, 0:n, :], x1_rows[t0 * P:(t0 + n) * P, :].rearrange(
                "(t p) f -> p t f", p=P)), e_x1in[s], ("e_x1", i))

        def e_load_choices(i):
            t0, n, s = e_first[i], E_TILES[i], i % E_SLOTS
            full = n if t0 + n < TILES else n - 1
            if i == 0:
                for j in range(SLOT_TILES - 3, SLOT_TILES):
                    D.wait(("yb_out", j))
            D.dma(lambda e: e.dma_start(
                e_ch[s][:, 0:full, :, :].rearrange("p t k f -> p t (k f)"),
                choice_rows[t0 * P * TOP_K:(t0 + full) * P * TOP_K, :].rearrange(
                    "(t p k) f -> p t (k f)", p=P, k=TOP_K)), e_chin[s],
                ("e_ch", i) if full == n else None)
            if full < n:
                V.wait(("E_y", e_first[i - E_SLOTS + 1] - 1))
                V.do(lambda e: e.memset(e_ch[s][:, n - 1, :, :], 0.0), "e_tail")
                D.wait("e_tail")
                D.dma(lambda e: e.dma_start(
                    e_ch[s][0:LAST_ROWS, n - 1, :, :].rearrange("p k f -> p (k f)"),
                    choice_rows[(TILES - 1) * P * TOP_K:NODES * TOP_K, :].rearrange(
                        "(p k) f -> p (k f)", k=TOP_K)), e_chin[s], ("e_ch", i))

        def e_shift(i):
            t0, n = e_first[i], E_TILES[i]
            inv_std("E", t0, n, rstd_y)
            V.wait(("E", "rstd", t0))
            V.do(lambda e: e.scalar_tensor_tensor(
                shift_y[:, t0:t0 + n], mean_var[:, t0:t0 + n, 0], -1.0, rstd_y[:, t0:t0 + n],
                ALU.mult, ALU.mult), ("E_shift", i))

        def e_y0(i):
            t0, n, s = e_first[i], E_TILES[i], i % E_SLOTS
            S.wait(("e_x1", i))
            for k in range(n):
                t = t0 + k
                S.do(lambda e, k=k, t=t: e.activation(e_y[s][:, k, :], e_x1[s][:, k, :], ACT.Identity,
                                                      bias=shift[:, t:t + 1], scale=rstd[:, t:t + 1]),
                     ("E_y0", t))

        def e_sum(i):
            t0, n, s = e_first[i], E_TILES[i], i % E_SLOTS
            V.wait(("e_ch", i), "weight1")
            for k in range(n + 3):
                if k < n:
                    t = t0 + k
                    V.wait(("E_y0", t))
                    V.do(lambda e, k=k, t=t: e.scalar_tensor_tensor(
                        e_y[s][:, k, :], e_ch[s][:, k, 0, :], weight[:, 0, t:t + 1], e_y[s][:, k, :],
                        ALU.mult, ALU.add), ("E_1", t))
                if 1 <= k <= n:
                    t = t0 + k - 1
                    V.wait(("E_1", t))
                    V.do(lambda e, k=k, t=t: e.scalar_tensor_tensor(
                        e_y[s][:, k - 1, :], e_ch[s][:, k - 1, 1, :], weight[:, 1, t:t + 1],
                        e_y[s][:, k - 1, :], ALU.mult, ALU.add), ("E_y", t))
                if 2 <= k <= n + 1:
                    t = t0 + k - 2
                    V.wait(("E_y", t))
                    V.do(lambda e, k=k, t=t: e.bn_stats(stats[:, t % BATCH, :], e_y[s][:, k - 2, :]),
                         ("E", "stats", t))
                if 3 <= k:
                    t = t0 + k - 3
                    V.wait(("E", "stats", t))
                    V.do(lambda e, t=t: e.bn_aggr(mean_var[:, t, :], stats[:, t % BATCH, :]),
                         ("E", "aggr", t))
                if k == 1 and i >= 1:
                    e_shift(i - 1)
            var_plus_eps("E", t0, n)

        pe_tiles, pe_bank, PE_BANKS = [], {}, 8

        def on_pe(k):
            return k % 2 == 1

        def e_finish(i):
            t0, n, s = e_first[i], E_TILES[i], i % E_SLOTS
            T.wait(("e_x1", i))
            G.wait(("e_x1", i))
            S.wait(("E_shift", i))
            for k in range(n):
                t = t0 + k
                S.do(lambda e, k=k, t=t: e.activation(
                    e_y[s][:, k, :], e_y[s][:, k, :], ACT.Identity, bias=shift_y[:, t:t + 1],
                    scale=rstd_y[:, t:t + 1]), ("E_n", t))
                if not on_pe(k):
                    G.wait(("E_y0", t))
                    G.do(lambda e, k=k: e.tensor_tensor(
                        e_x1[s][:, k, :], e_x1[s][:, k, :], beta_bc[:, :], ALU.add), ("E_x1b", t))
                G.wait(("E_n", t))
                G.do(lambda e, k=k: e.tensor_tensor(e_y[s][:, k, :], e_y[s][:, k, :], gamma_bc[:, :],
                                                    ALU.mult), ("E_g", t))
                if on_pe(k):
                    if len(pe_tiles) >= PE_BANKS:
                        T.wait(("E_out", pe_tiles[-PE_BANKS]))
                    pe_bank[t] = bank[len(pe_tiles) % PE_BANKS]
                    pe_tiles.append(t)
                    terms = ((ones[0:1, :], beta_bc[0:1, :]), (ident[:, :], e_x1[s][:, k, :]),
                             (ident[:, :], e_y[s][:, k, :]))
                    for m, (left, right) in enumerate(terms):
                        if m == 2:
                            T.wait(("E_g", t))
                        T.do(lambda e, t=t, m=m, left=left, right=right: e.matmul(
                            pe_bank[t][:, 0:F_IN], left, right, start=(m == 0), stop=(m == 2)),
                            ("E_mm", t) if m == 2 else None)

        def e_store(i):
            t0, n, s = e_first[i], E_TILES[i], i % E_SLOTS
            full = n if t0 + n < TILES else n - 1
            for k in range(n):
                t = t0 + k
                if on_pe(k):
                    S.wait(("E_mm", t))
                    S.do(copy_s(e_x1[s][:, k, :], pe_bank[t][:, 0:F_IN]), ("E_out", t))
                else:
                    V.wait(("E_g", t), ("E_x1b", t))
                    V.do(lambda e, k=k: e.tensor_tensor(e_x1[s][:, k, :], e_x1[s][:, k, :],
                                                        e_y[s][:, k, :], ALU.add), ("E_out", t))
            for pe in (False, True):
                D.wait(("E_out", t0 + max(k for k in range(n) if on_pe(k) == pe)))
            D.dma(lambda e: e.dma_start(
                out[t0 * P:(t0 + full) * P, :].rearrange("(t p) f -> p t f", p=P), e_x1[s][:, 0:full, :]),
                out_d[s], ("out", i) if full == n else None)
            if full < n:
                D.dma(lambda e: e.dma_start(out[(TILES - 1) * P:NODES, :], e_x1[s][0:LAST_ROWS, n - 1, :]),
                      out_d[s], ("out", i))

        T.wait(("D_y", SLOT_TILES - 1), ("D_y", SLOT_TILES - 2), ("D_ht", SLOT_TILES - 1))
        LAST_E = len(E_TILES) - 1
        for i in range(2):
            e_load_x1(i)
        for i in range(2):
            e_load_choices(i)
        for i in range(2, E_SLOTS):
            e_load_x1(i)
            e_load_choices(i)
        e_y0(0)
        e_y0(1)
        e_sum(0)
        root("E", 0, E_TILES[0])
        for i in range(LAST_E + 1):
            if i < LAST_E:
                e_sum(i + 1)
            else:
                e_shift(i)
            e_finish(i)
            if i + 2 <= LAST_E:
                e_y0(i + 2)
            e_store(i)
            if i < LAST_E:
                root("E", e_first[i + 1], E_TILES[i + 1])
            if i + E_SLOTS <= LAST_E:
                e_load_x1(i + E_SLOTS)
                e_load_choices(i + E_SLOTS)
        for i in range(LAST_E + 1 - E_SLOTS, LAST_E + 1):
            D.wait(("out", i))

        block = ctx.enter_context(nc.Block())

        @block.sync
        def _(eng):
            D.emit(eng)

        @block.scalar
        def _(eng):
            S.emit(eng)

        @block.gpsimd
        def _(eng):
            G.emit(eng)

        @block.tensor
        def _(eng):
            T.emit(eng)

        @block.vector
        def _(eng):
            V.emit(eng)


_INS = ["x", "src", "dst", "L0_gnn_W", "L0_gnn_a_src", "L0_gnn_a_dst", "L0_ffn_gate_w", "L0_ffn_gate_b",
        "L0_ffn_w1", "L0_ffn_b1", "L0_ffn_w2", "L0_ffn_b2", "L0_ffn_gamma", "L0_ffn_beta"]


def kernel(**inputs):
    import numpy as _np
    import concourse.bacc as _bacc
    from concourse import mybir as _mybir
    from concourse.bass_utils import run_bass_kernel_spmd as _run

    nc = _bacc.Bacc("TRN2", target_bir_lowering=False, num_devices=1)
    arrays, args = {}, []
    for name in _INS:
        a = _np.ascontiguousarray(inputs[name])
        arrays[f"in_{name}"] = a
        args.append(nc.dram_tensor(f"in_{name}", a.shape, _mybir.dt.from_np(a.dtype), kind="ExternalInput").ap())
    args.append(nc.dram_tensor("out", (NODES, F_IN), _mybir.dt.float32, kind="ExternalOutput").ap())
    build_program(nc, *args)
    r = _run(nc, [arrays], core_ids=[0])
    return r.results[0]["out"]
```
